# Optimizing a Trainium2 kernel written in Bass

```python
import numpy as np
import jax
import jax.numpy as jnp

def _softmax(x, axis=-1):
    return jax.nn.softmax(x, axis=axis)

def _gelu(x):
    return jax.nn.gelu(x, approximate=True)

def _silu(x):
    return jax.nn.silu(x)

def _sigmoid(x):
    return jax.nn.sigmoid(x)

def _layernorm(x, axis=-1, eps=1e-05):
    m = jnp.mean(x, axis=axis, keepdims=True)
    v = jnp.var(x, axis=axis, keepdims=True)
    return (x - m) / jnp.sqrt(v + eps)

def _scatter_add(tgt, idx, src, axis=0):
    return tgt.at[idx].add(src)

def _segment_sum(src, seg, n):
    return jax.ops.segment_sum(src, seg, n)
kernel_name = 'mk_adj_resnorm_d4_adj_r2_f98e9a'

def setup_inputs(seed: int=0):
    np.random.seed(seed)
    _w = jnp.asarray

    def _rec_inputs():
        import jax
        import jax.numpy as jnp
        _gk = jax.random.key(seed)
        x = 0.0002279 + 0.9999 * jax.random.normal(jax.random.fold_in(_gk, 1), (8192, 128), jnp.float32)
        _a = jax.random.bernoulli(jax.random.fold_in(_gk, 2), 0.000488281, (8192, 8192))
        adj = _a.astype(jnp.int32)
        return (x, adj)
    x, adj = _rec_inputs()

    def _L0_gnn_setup():
        import jax, jax.numpy as jnp
        import numpy as np
        N, D = (4096, 128)
        key = jax.random.key(seed)
        k1, k2, k3 = jax.random.split(key, 3)
        adj = jax.random.randint(k1, (N, N), 0, 2, dtype=jnp.int32)
        emb = jax.random.normal(k2, (N, D), dtype=jnp.float32)
        attn = jax.random.normal(k3, (2 * D, 1), dtype=jnp.float32)
        return {'adj': adj, 'emb': emb, 'attn': attn}
    _L0_gnn_all = _L0_gnn_setup()
    _L0_gnn_in = {k: v for k, v in _L0_gnn_all.items() if k in ('attn',)}
    del _L0_gnn_all

    def _L1_gnn_setup():
        import jax, jax.numpy as jnp
        import numpy as np
        NEG_INF = -1000000000.0
        key = jax.random.key(seed)
        k1, k2, k3, k4 = jax.random.split(key, 4)
        N, Fin, Fout = (4096, 128, 128)
        h = jax.random.normal(k1, (N, Fin), dtype=jnp.float32)
        adj = jax.random.randint(k2, (N, N), 0, 2, dtype=jnp.int32)
        W = jax.random.normal(k3, (Fin, Fout), dtype=jnp.float32) * (1.0 / np.sqrt(Fin))
        a = jax.random.normal(k4, (2 * Fout,), dtype=jnp.float32) * (1.0 / np.sqrt(2 * Fout))
        return {'h': h, 'adj': adj, 'W': W, 'a': a}
    _L1_gnn_all = _L1_gnn_setup()
    _L1_gnn_in = {k: v for k, v in _L1_gnn_all.items() if k in ('W', 'a')}
    del _L1_gnn_all

    def _L2_gnn_setup():
        import jax, jax.numpy as jnp
        import numpy as np
        NUM_NODES = 3072
        INPUT_DIM = 128
        OUTPUT_DIM = 128
        NUM_HEADS = 4
        HEAD_DIM = OUTPUT_DIM // NUM_HEADS
        NEG_INF = -9000000000000000.0
        key = jax.random.key(seed)
        k_x, k_adj, k_W, k_a = jax.random.split(key, 4)
        x = jax.random.normal(k_x, (NUM_NODES, INPUT_DIM), dtype=jnp.float32)
        adj = jax.random.randint(k_adj, (NUM_NODES, NUM_NODES), 0, 2, dtype=jnp.int32)
        W = jax.random.uniform(k_W, (NUM_HEADS, INPUT_DIM, HEAD_DIM), dtype=jnp.float32, minval=-1.0, maxval=1.0) * np.sqrt(6.0 / INPUT_DIM)
        a = jax.random.uniform(k_a, (NUM_HEADS, 2 * HEAD_DIM, 1), dtype=jnp.float32, minval=-1.0, maxval=1.0) * np.sqrt(6.0 / (2 * HEAD_DIM))
        return {'x': x, 'adj': adj, 'W': W, 'a': a}
    _L2_gnn_all = _L2_gnn_setup()
    _L2_gnn_in = {k: v for k, v in _L2_gnn_all.items() if k in ('W', 'a')}
    del _L2_gnn_all

    def _L3_gnn_setup():
        import jax, jax.numpy as jnp
        import numpy as np
        N = 6144
        IN_DIM = 128
        OUT_DIM = 128
        LR_SLOPE = 0.01
        NEG_INF = -9e+16
        key = jax.random.key(seed)
        k1, k2, k3, k4 = jax.random.split(key, 4)
        emb_mat = jax.random.normal(k1, (N, IN_DIM), dtype=jnp.float32)
        adj_mat = jax.random.randint(k2, (N, N), 0, 2, dtype=jnp.int32)
        W = jax.random.normal(k3, (OUT_DIM, IN_DIM), dtype=jnp.float32) * (2.0 / (IN_DIM + OUT_DIM)) ** 0.5
        a = jax.random.normal(k4, (2 * OUT_DIM, 1), dtype=jnp.float32) * (2.0 / (2 * OUT_DIM + 1)) ** 0.5
        return {'emb_mat': emb_mat, 'adj_mat': adj_mat, 'W': W, 'a': a}
    _L3_gnn_all = _L3_gnn_setup()
    _L3_gnn_in = {k: v for k, v in _L3_gnn_all.items() if k in ('W', 'a')}
    del _L3_gnn_all
    return {'x': x, 'adj': adj, 'L0_gnn_attn': _L0_gnn_in['attn'], 'L1_gnn_W': _L1_gnn_in['W'], 'L1_gnn_a': _L1_gnn_in['a'], 'L2_gnn_W': _L2_gnn_in['W'], 'L2_gnn_a': _L2_gnn_in['a'], 'L3_gnn_W': _L3_gnn_in['W'], 'L3_gnn_a': _L3_gnn_in['a']}

def reference(x, adj, L0_gnn_attn, L1_gnn_W, L1_gnn_a, L2_gnn_W, L2_gnn_a, L3_gnn_W, L3_gnn_a):
    import jax
    import jax.numpy as jnp

    def _L0_gnn_ref(adj, emb, attn):
        import jax, jax.numpy as jnp
        import numpy as np
        N, D = (4096, 128)
        d = emb.shape[1]
        s_i = emb @ attn[:d]
        s_j = emb @ attn[d:]
        e = jax.nn.leaky_relu(s_i + s_j.T, negative_slope=0.2)
        neg_inf = jnp.float32(-1000000000.0)
        e = e + jnp.where(adj > 0, jnp.float32(0.0), neg_inf)
        alpha = jax.nn.softmax(e, axis=1)
        return alpha @ emb

    def _L1_gnn_ref(h, adj, W, a):
        import jax, jax.numpy as jnp
        import numpy as np
        NEG_INF = -1000000000.0
        Fout = W.shape[1]
        Wh = h @ W
        a1, a2 = (a[:Fout], a[Fout:])
        s_key = Wh @ a1
        s_qry = Wh @ a2
        e = jax.nn.leaky_relu(s_qry[:, None] + s_key[None, :], negative_slope=0.2)
        scores = jnp.where(adj > 0, e, jnp.float32(NEG_INF))
        attention = jax.nn.softmax(scores, axis=1)
        h_prime = attention @ Wh
        return jax.nn.elu(h_prime)

    def _L2_gnn_ref(x, adj, W, a):
        import jax, jax.numpy as jnp
        import numpy as np
        NUM_NODES = 3072
        INPUT_DIM = 128
        OUTPUT_DIM = 128
        NUM_HEADS = 4
        HEAD_DIM = OUTPUT_DIM // NUM_HEADS
        NEG_INF = -9000000000000000.0
        H, Din, d = W.shape
        N = x.shape[0]
        h = jnp.einsum('ni,hid->hnd', x, W)
        a_dst = a[:, :d, 0]
        a_src = a[:, d:, 0]
        s_dst = jnp.einsum('hnd,hd->hn', h, a_dst)
        s_src = jnp.einsum('hnd,hd->hn', h, a_src)
        energy = jax.nn.leaky_relu(s_src[:, :, None] + s_dst[:, None, :], negative_slope=0.2)
        energy = jnp.where(adj[None] > 0, energy, NEG_INF)
        attention = jax.nn.softmax(energy, axis=-1)
        h_prime = jnp.einsum('hij,hjd->hid', attention, h)
        return jnp.reshape(h_prime, (N, H * d))

    def _L3_gnn_ref(emb_mat, adj_mat, W, a):
        import jax, jax.numpy as jnp
        import numpy as np
        N = 6144
        IN_DIM = 128
        OUT_DIM = 128
        LR_SLOPE = 0.01
        NEG_INF = -9e+16
        out_dim = W.shape[0]
        e_new = emb_mat @ W.T
        a1 = a[:out_dim, :]
        a2 = a[out_dim:, :]
        source_scores = e_new @ a1
        target_scores = e_new @ a2
        e = source_scores + target_scores.T
        e = jax.nn.leaky_relu(e, negative_slope=LR_SLOPE)
        e = jnp.where(adj_mat > 0, e, NEG_INF)
        attention = jax.nn.softmax(e, axis=-1)
        e_transf = attention @ e_new
        return jax.nn.relu(e_transf)
    x = _layernorm(x + _L0_gnn_ref(adj, x, L0_gnn_attn), axis=-1)
    x = _layernorm(x + _L1_gnn_ref(x, adj, L1_gnn_W, L1_gnn_a), axis=-1)
    x = _layernorm(x + _L2_gnn_ref(x, adj, L2_gnn_W, L2_gnn_a), axis=-1)
    x = _layernorm(x + _L3_gnn_ref(x, adj, L3_gnn_W, L3_gnn_a), axis=-1)
    return x

_drawn_inputs = setup_inputs


def setup_inputs(seed=0):
    import zlib

    import numpy as np

    out = dict(_drawn_inputs(seed))
    spreads = {}
    factors = {}
    for name, (base, spread) in spreads.items():
        noise = np.random.default_rng([zlib.crc32(name.encode()), seed]).standard_normal(out[name].shape)
        drawn = base * np.exp(spread * noise) if base else spread * noise
        out[name] = jnp.asarray(drawn.astype(out[name].dtype))
    for name, factor in factors.items():
        out[name] = (out[name] * factor).astype(out[name].dtype)
    return out
```

```python
import concourse.bass as bass
from concourse import mybir
from contextlib import ExitStack

f32 = mybir.dt.float32
i32 = mybir.dt.int32
ALU = mybir.AluOpType
ACT = mybir.ActivationFunctionType
AX = mybir.AxisListType

N = 8192
D = 128
T = N // D
KEY, QRY = D, D + 4
WX = D + 8
EPS = 1e-5
LAYERS = [(1, 0.2, -1e9), (1, 0.2, -1e9), (4, 0.2, -9e15), (1, 0.01, -9e16)]
GRP = 4


class Chain:

    def __init__(self, eng, sem):
        self.eng, self.sem, self.base, self.count = eng, sem, 0, 0

    def loop(self, i, per):
        self.start, self.per = self.count, per
        self.base = i * per

    def endloop(self, trips):
        assert self.count - self.start == self.per, (self.count - self.start, self.per)
        self.base, self.count = 0, self.start + self.per * trips

    def link(self, ins):
        self.count += 1
        ins.then_inc(self.sem, 1)
        self.eng.wait_ge(self.sem, self.base + self.count)


def build_program(nc, x, adj, L0_attn, L1_W, L1_a, L2_W, L2_a, L3_W, L3_a, out):
    ctx = ExitStack()
    with ctx:
        def sb(name, shape, dt=f32):
            return ctx.enter_context(nc.sbuf_tensor(name, shape, dt))

        def pb(name, shape, dt=f32):
            return ctx.enter_context(nc.psum_tensor(name, shape, dt))

        def sem(name):
            return ctx.enter_context(nc.semaphore(name))

        ident = sb("ident", [D, D])
        ones = sb("ones", [D, D])
        zeros = sb("zeros", [D, D])
        Wext = sb("Wext", [D, 4, WX])
        W2nat = sb("W2nat", [D, D])
        WT = sb("WT", [D, 2, D])
        A1 = sb("A1", [D, 2])
        A2 = sb("A2", [D, 8])
        A3 = sb("A3", [D, 2])
        X = sb("X", [D, T, D])
        AG = sb("AG", [D, T, D])
        WH = sb("WH", [D, T, WX])
        KB = sb("KB", [D, N])
        E = sb("E", [D, N])
        A = sb("A", [D, N], i32)
        PT = sb("PT", [D, 2, GRP * D])
        xT = PT[:, 0, 0:D]
        diag = PT[:, 1, 0:D]
        xs = PT[:, 0, D:2 * D]
        small = sb("small", [D, 16])

        psA = pb("psA", [D, 512])
        psB = pb("psB", [D, 512])
        psT = [pb(f"psT{i}", [D, 512]) for i in range(2)]
        acc = pb("acc", [D, 512])

        s_load = sem("setup_loads")
        s_id = sem("identity_ready")
        s_zero = sem("weights_zeroed")
        s_wt = sem("weights_transposed")
        s_wtc = sem("transposes_copied")
        s_wa = sem("score_weights_ready")
        s_setup = sem("setup_done")

        d_x = sem("dense_x_loaded")
        d_xs = sem("dense_x_staged")
        d_xT = sem("dense_x_transposed")
        d_xTc = sem("dense_xT_copied")
        d_pr = sem("dense_projected")
        d_wh = sem("dense_projection_copied")
        d_diag = sem("dense_diag_ready")
        d_kb = sem("dense_keys_spread")
        d_kbc = sem("dense_keys_copied")
        d_adj = sem("dense_adj_loaded")
        d_e = sem("dense_scores_ready")
        d_p = sem("dense_probs_ready")
        d_tr = sem("dense_probs_transposed")
        d_pt = sem("dense_PT_copied")
        d_mm = sem("dense_group_multiplied")
        d_out = sem("dense_tile_normed")
        d_el = sem("dense_elu_exp")
        d_bh = sem("dense_rows_regrouped")
        d_ex = sem("dense_elu_exp_ready")
        d_var = sem("dense_variance_ready")
        d_ln = sem("dense_log_ready")
        d_rs = sem("dense_rstd_ready")
        d_lay = sem("dense_layer_done")
        d_ch = sem("dense_dve_chain")
        d_store = sem("dense_out_stored")

        with nc.Block() as block:
            @block.gpsimd
            def _(pool):
                nc.gpsimd.memset(ident[:], 1.0).then_inc(s_zero, 1)
                nc.gpsimd.memset(ones[:], 1.0).then_inc(s_zero, 1)
                nc.gpsimd.memset(zeros[:], 0.0).then_inc(s_zero, 1)
                nc.gpsimd.memset(A2[:], 0.0).then_inc(s_zero, 1)
                nc.gpsimd.memset(Wext[:], 0.0).then_inc(s_zero, 1)
                pool.wait_ge(s_zero, 5)
                nc.gpsimd.affine_select(out=ident[:], in_=ident[:], compare_op=ALU.is_equal, fill=0.0, base=0,
                                        pattern=[[-1, D]], channel_multiplier=1).then_inc(s_id, 1)

            @block.sync
            def _(sp):
                sp.wait_ge(s_zero, 5)
                sp.dma_start(Wext[:, 0, KEY:KEY + 1], L0_attn[D:2 * D, :]).then_inc(s_load, 16)
                sp.dma_start(Wext[:, 0, QRY:QRY + 1], L0_attn[0:D, :]).then_inc(s_load, 16)
                sp.dma_start(Wext[:, 1, 0:D], L1_W).then_inc(s_load, 16)
                for k in range(2):
                    rows = slice(k * D, (k + 1) * D)
                    sp.dma_start(A1[:, k:k + 1], L1_a[rows].rearrange("(p o) -> p o", o=1)).then_inc(s_load, 16)
                    sp.dma_start(A3[:, k:k + 1], L3_a[rows, :]).then_inc(s_load, 16)
                sp.dma_start(Wext[:, 2, 0:D].rearrange("i (h d) -> i h d", h=4),
                             L2_W.rearrange("h i d -> i h d")).then_inc(s_load, 16)
                for h in range(4):
                    rows = slice(32 * h, 32 * h + 32)
                    sp.dma_start(A2[rows, h:h + 1], L2_a[h, 0:32, :]).then_inc(s_load, 16)
                    sp.dma_start(A2[rows, 4 + h:5 + h], L2_a[h, 32:64, :]).then_inc(s_load, 16)
                sp.dma_start(W2nat[:], L3_W).then_inc(s_load, 16)

            @block.tensor
            def _(pe):
                pe.wait_ge(s_id, 1)
                pe.wait_ge(s_load, 17 * 16)
                nc.tensor.transpose(psA[:, 0:D], Wext[:, 1, 0:D], ident[:])
                nc.tensor.transpose(psA[:, D:2 * D], Wext[:, 2, 0:D], ident[:])
                nc.tensor.transpose(psA[:, 2 * D:3 * D], W2nat[:], ident[:]).then_inc(s_wt, 1)
                pe.wait_ge(s_wtc, 1)
                nc.tensor.matmul(psB[:, 0:2], WT[:, 0, :], A1[:], start=True, stop=True)
                nc.tensor.matmul(psB[:, 8:16], WT[:, 1, :], A2[:], start=True, stop=True)
                nc.tensor.matmul(psB[:, 16:18], W2nat[:], A3[:], start=True, stop=True).then_inc(s_wa, 1)

            @block.vector
            def _(dve):
                dve.wait_ge(s_wt, 1)
                nc.vector.tensor_copy(WT[:, :, :], psA[:, 0:2 * D].rearrange("p (k d) -> p k d", k=2)).then_inc(s_wtc, 1)
                nc.vector.tensor_copy(Wext[:, 3, 0:D], psA[:, 2 * D:3 * D])
                nc.vector.tensor_copy(Wext[:, 0, 0:D], ident[:])
                dve.wait_ge(s_wa, 1)
                nc.vector.tensor_copy(Wext[:, 1, KEY:KEY + 1], psB[:, 0:1])
                nc.vector.tensor_copy(Wext[:, 1, QRY:QRY + 1], psB[:, 1:2])
                nc.vector.tensor_copy(Wext[:, 2, KEY:KEY + 8], psB[:, 8:16])
                nc.vector.tensor_copy(Wext[:, 3, QRY:QRY + 1], psB[:, 16:17])
                nc.vector.tensor_copy(Wext[:, 3, KEY:KEY + 1], psB[:, 17:18]).then_inc(s_setup, 1)
                dve.wait_ge(s_setup, 1)

        passes = [(l, h) for l, (heads, _, _) in enumerate(LAYERS) for h in range(heads)]
        GROUPS = T // GRP
        HEADS_END = sum(heads for heads, _, _ in LAYERS[:3]) - 1
        by_head = nc.dram_tensor("sums_by_head", (4, N, D // 4), f32).ap()
        LAY_LINKS = [0, 6, 0, 1]

        def dense_sync(sp):
            sp.dma_start(X[:], x.rearrange("(t p) d -> p t d", p=D)).then_inc(d_x, 16)
            for n in range(len(passes)):
                if n:
                    sp.wait_ge(d_e, n * T)
                sp.dma_start(A[:], adj[0:D, :]).then_inc(d_adj, 16)
                with sp.Fori(1, T) as t:
                    sp.wait_ge(d_e, t + n * T)
                    sp.dma_start(A[:], adj.rearrange("(t p) j -> t p j", p=D)[bass.ds(t, 1), :, :].rearrange("o p j -> p (o j)")).then_inc(d_adj, 16)
                if n == HEADS_END:
                    sp.wait_ge(d_out, (n + 1) * T)
                    heads = LAYERS[2][0]
                    for h in range(heads):
                        sp.dma_start(by_head.rearrange("h (t p) d -> h p t d", p=D)[h],
                                     AG[:, :, h * (D // heads):(h + 1) * (D // heads)]).then_inc(d_bh, 16)
                    sp.wait_ge(d_bh, 16 * heads)
                    sp.dma_start(AG[:], by_head.rearrange("h (m k) d -> (h m) (k d)", k=heads)
                                 .rearrange("(t p) f -> p t f", p=D)).then_inc(d_bh, 16)
            sp.wait_ge(d_lay, len(LAYERS))
            sp.dma_start(out.rearrange("(t p) d -> p t d", p=D), X[:]).then_inc(d_store, 16)
            sp.wait_ge(d_store, 16)

        def dense_tensor(pe):
            n = 0
            for l, (heads, _, _) in enumerate(LAYERS):
                with pe.Fori(0, T) as t:
                    pe.wait_ge(d_xs, t + (l * T + 1))
                    nc.tensor.transpose(psA[:, 0:D], xs, ident[:]).then_inc(d_xT, 1)
                    pe.wait_ge(d_xTc, t + (l * T + 1))
                    nc.tensor.matmul(psB[:, 0:WX], xT, Wext[:, l, :], start=True, stop=True).then_inc(d_pr, 1)
                    pe.wait_ge(d_wh, t + (l * T + 1))
                for h in range(heads):
                    dh = D // heads
                    with pe.Fori(0, T) as t:
                        pe.wait_ge(d_diag, t + (n * T + 1))
                        nc.tensor.matmul(psA[:, 0:D], ones[:], diag, start=True, stop=True).then_inc(d_kb, 1)
                        pe.wait_ge(d_kbc, t + (n * T + 1))
                    with pe.Fori(0, T) as t:
                        pe.wait_ge(d_p, t + (n * T + 1))
                        if n:
                            pe.wait_ge(d_out, t + n * T)
                        else:
                            pe.wait_ge(d_kbc, T)
                        for g in range(GROUPS):
                            for j in range(g * GRP, (g + 1) * GRP):
                                last = nc.tensor.transpose(psT[g % 2][:, j % GRP * D:(j % GRP + 1) * D],
                                                           E[:, j * D:(j + 1) * D], ident[:])
                            last.then_inc(d_tr, 1)
                            pe.wait_ge(d_pt, t * GROUPS + (n * T * GROUPS + g + 1))
                            for j in range(g * GRP, (g + 1) * GRP):
                                last = nc.tensor.matmul(acc[:, 0:dh], PT[:, g % 2, j % GRP * D:(j % GRP + 1) * D],
                                                        WH[:, j, h * dh:(h + 1) * dh],
                                                        start=(j == 0), stop=(j == T - 1))
                            last.then_inc(d_mm, 1)
                    n += 1

        def dense_scalar(act):
            n = 0
            for l, (heads, _, _) in enumerate(LAYERS):
                if l:
                    act.wait_ge(d_lay, l)
                else:
                    act.wait_ge(d_x, 16)
                with act.Fori(0, T) as t:
                    nc.scalar.copy(xs, X[:, bass.ds(t, 1), :].rearrange("p o d -> p (o d)")).then_inc(d_xs, 1)
                    act.wait_ge(d_xT, t + (l * T + 1))
                    nc.scalar.copy(xT, psA[:, 0:D]).then_inc(d_xTc, 1)
                    act.wait_ge(d_pr, t + (l * T + 1))
                    nc.scalar.copy(WH[:, bass.ds(t, 1), :].rearrange("p o d -> p (o d)"), psB[:, 0:WX]).then_inc(d_wh, 1)
                for h in range(heads):
                    with act.Fori(0, T) as t:
                        act.wait_ge(d_kb, t + (n * T + 1))
                        nc.scalar.copy(KB[:, bass.ds(t * D, D)], psA[:, 0:D]).then_inc(d_kbc, 1)
                    with act.Fori(0, T) as t:
                        act.wait_ge(d_e, t + (n * T + 1))
                        nc.scalar.activation(E[:], E[:], ACT.Exp, bias=small[:, 1:2], accum_out=small[:, 2:3]).then_inc(d_p, 1)
                        with act.Fori(0, GROUPS // 2) as g:
                            for b in range(2):
                                at = t * GROUPS + g * 2 + (n * T * GROUPS + b)
                                act.wait_ge(d_tr, at + 1)
                                nc.scalar.copy(PT[:, b, :], psT[b][:]).then_inc(d_pt, 1)
                    n += 1
                with act.Fori(0, T) as t:
                    if l == 1:
                        act.wait_ge(d_el, t + 1)
                        nc.scalar.activation(E[:, 0:D], E[:, 0:D], ACT.Exp).then_inc(d_ex, 1)
                    act.wait_ge(d_var, t + (l * T + 1))
                    nc.scalar.activation(small[:, 9:10], small[:, 8:9], ACT.Ln).then_inc(d_ln, 1)
                    act.wait_ge(d_ln, t + (l * T + 1))
                    nc.scalar.activation(small[:, 8:9], small[:, 9:10], ACT.Exp, scale=-0.5).then_inc(d_rs, 1)

        def dense_vector(dve):
            ch = Chain(dve, d_ch)
            n = 0
            for l, (heads, slope, neg) in enumerate(LAYERS):
                dve.wait_ge(d_wh, (l + 1) * T)
                for h in range(heads):
                    dh = D // heads
                    with dve.Fori(0, T) as t:
                        if n:
                            dve.wait_ge(d_kbc, t + n * T)
                            dve.wait_ge(d_mm, n * T * GROUPS)
                        else:
                            dve.wait_ge(d_xTc, T)
                        nc.vector.tensor_scalar(diag, ident[:], WH[:, bass.ds(t, 1), KEY + h:KEY + h + 1].rearrange("p o d -> p (o d)"),
                                                None, ALU.mult).then_inc(d_diag, 1)
                        dve.wait_ge(d_kb, t + (n * T + 1))
                    dve.wait_ge(d_kbc, (n + 1) * T)
                    with dve.Fori(0, T) as t:
                        ch.loop(t, 9 if l else 8)
                        ch.link(nc.vector.tensor_scalar(E[:], KB[:], WH[:, bass.ds(t, 1), QRY + h:QRY + h + 1].rearrange("p o d -> p (o d)"),
                                                        None, ALU.add))
                        ch.link(nc.vector.scalar_tensor_tensor(out=E[:], in0=E[:], scalar=slope, in1=E[:], op0=ALU.mult, op1=ALU.max))
                        dve.wait_ge(d_adj, t * 16 + (n * T + 1) * 16)
                        M = A[:].bitcast(f32)
                        ch.link(nc.vector.tensor_scalar(M, A[:], 0.0, None, ALU.is_gt))
                        if l:
                            ch.link(nc.vector.tensor_tensor(E[:], E[:], M, ALU.mult))
                        ch.link(nc.vector.tensor_scalar(M, M, 1.0, -neg, ALU.subtract, ALU.mult))
                        ch.link(nc.vector.tensor_tensor(E[:], E[:], M, ALU.add))
                        ch.link(nc.vector.reduce_max(small[:, 0:1], E[:], AX.X))
                        nc.vector.tensor_scalar(small[:, 1:2], small[:, 0:1], -1.0, None, ALU.mult).then_inc(d_e, 1)
                        dve.wait_ge(d_mm, t * GROUPS + (n * T + 1) * GROUPS)
                        ch.link(nc.vector.reciprocal(small[:, 3:4], small[:, 2:3]))
                        ch.link(nc.vector.tensor_scalar(AG[:, bass.ds(t, 1), h * dh:(h + 1) * dh].rearrange("p o d -> p (o d)"),
                                                        acc[:, 0:dh], small[:, 3:4], None, ALU.mult))
                        nc.vector.tensor_copy(small[:, 4:5], small[:, 3:4]).then_inc(d_out, 1)
                        ch.endloop(T)
                    n += 1
                if l == 2:
                    dve.wait_ge(d_bh, 16 * (heads + 1))
                with dve.Fori(0, T) as t:
                    ag = AG[:, bass.ds(t, 1), :].rearrange("p o d -> p (o d)")
                    xt = X[:, bass.ds(t, 1), :].rearrange("p o d -> p (o d)")
                    ch.loop(t, {0: 0, 1: 3, 2: 0, 3: 1}[l] + 7)
                    if l == 1:
                        nc.vector.tensor_scalar(E[:, 0:D], ag, 0.0, None, ALU.min).then_inc(d_el, 1)
                        ch.link(nc.vector.tensor_scalar(ag, ag, 0.0, None, ALU.max))
                        dve.wait_ge(d_ex, t + 1)
                        ch.link(nc.vector.tensor_scalar(E[:, 0:D], E[:, 0:D], 1.0, None, ALU.subtract))
                        ch.link(nc.vector.tensor_tensor(ag, ag, E[:, 0:D], ALU.add))
                    if l == 3:
                        ch.link(nc.vector.tensor_scalar(ag, ag, 0.0, None, ALU.max))
                    xw = E[:, D:2 * D]
                    ch.link(nc.vector.tensor_tensor(xw, xt, ag, ALU.add))
                    ch.link(nc.vector.reduce_sum(small[:, 6:7], xw, AX.X))
                    ch.link(nc.vector.tensor_scalar(small[:, 6:7], small[:, 6:7], 1.0 / D, None, ALU.mult))
                    ch.link(nc.vector.tensor_scalar(xw, xw, small[:, 6:7], None, ALU.subtract))
                    ch.link(nc.vector.tensor_tensor(E[:, 0:D], xw, xw, ALU.mult))
                    ch.link(nc.vector.reduce_sum(small[:, 7:8], E[:, 0:D], AX.X))
                    nc.vector.tensor_scalar(small[:, 8:9], small[:, 7:8], 1.0 / D, EPS, ALU.mult, ALU.add).then_inc(d_var, 1)
                    dve.wait_ge(d_rs, t + (l * T + 1))
                    ch.link(nc.vector.tensor_scalar(xt, xw, small[:, 8:9], None, ALU.mult))
                    ch.endloop(T)
                nc.vector.tensor_copy(small[:, 10:11], small[:, 8:9]).then_inc(d_lay, 1)

        with nc.Block() as block:
            @block.sync
            def _(sp):
                dense_sync(sp)

            @block.tensor
            def _(pe):
                dense_tensor(pe)

            @block.scalar
            def _(act):
                dense_scalar(act)

            @block.vector
            def _(dve):
                dense_vector(dve)


_INS = ['x', 'adj', 'L0_gnn_attn', 'L1_gnn_W', 'L1_gnn_a', 'L2_gnn_W', 'L2_gnn_a', 'L3_gnn_W', 'L3_gnn_a']
_OUTS = [((8192, 128), 'float32')]


def kernel(**inputs):
    import numpy as _np
    import concourse.bacc as _bacc
    from concourse import mybir as _mybir
    from concourse.bass_utils import run_bass_kernel_spmd as _run

    nc = _bacc.Bacc("TRN2", target_bir_lowering=False, num_devices=1)
    arrays, args = {}, []
    for name in _INS:
        a = _np.ascontiguousarray(inputs[name])
        arrays[f"in_{name}_dram"] = a
        args.append(nc.dram_tensor(f"in_{name}_dram", a.shape, _mybir.dt.from_np(a.dtype), kind="ExternalInput").ap())
    for i, (shape, dtype) in enumerate(_OUTS):
        dt = _mybir.dt.from_np(_np.dtype(dtype))
        args.append(nc.dram_tensor(f"out_{i}_dram", shape, dt, kind="ExternalOutput").ap())
    build_program(nc, *args)
    r = _run(nc, [arrays], core_ids=[0])
    got = tuple(r.results[0][f"out_{i}_dram"] for i in range(len(_OUTS)))
    return got[0]
```

```python
import concourse.bass as bass
from concourse import mybir
from contextlib import ExitStack

f32 = mybir.dt.float32
f16 = mybir.dt.float16
i32 = mybir.dt.int32
ALU = mybir.AluOpType
ACT = mybir.ActivationFunctionType
AX = mybir.AxisListType

N = 8192
D = 128
T = N // D
KEY, QRY = D, D + 4
WX = D + 8
EPS = 1e-5
LAYERS = [(1, 0.2, -1e9), (1, 0.2, -1e9), (4, 0.2, -9e15), (1, 0.01, -9e16)]
SLOTS = 16
CH = 1024
NCH = N // CH
PROFILE = [(1, 16), (1, 8), (2, 7), (4, 6), (5, 5), (6, 4), (6, 3), (5, 2), (2, 1)]
ROOM = [s for n, s in PROFILE for _ in range(n)]
PAIRS = T // 2
assert len(ROOM) == PAIRS
BIG = 1e30
TW = D + 4
RW = D + 20
R_ONE, R_SLOT, R_QRY, R_ID = D, D + 1, D + 17, D + 18
FORCE = None
GRP = 4


class Chain:

    def __init__(self, eng, sem):
        self.eng, self.sem, self.base, self.count = eng, sem, 0, 0

    def loop(self, i, per):
        self.start, self.per = self.count, per
        self.base = i * per

    def endloop(self, trips):
        assert self.count - self.start == self.per, (self.count - self.start, self.per)
        self.base, self.count = 0, self.start + self.per * trips

    def add(self, ins):
        self.count += 1
        ins.then_inc(self.sem, 1)

    def wait(self):
        self.eng.wait_ge(self.sem, self.base + self.count)

    def link(self, ins):
        self.add(ins)
        self.wait()


def build_program(nc, x, adj, L0_attn, L1_W, L1_a, L2_W, L2_a, L3_W, L3_a, out):
    ctx = ExitStack()
    with ctx:
        def sb(name, shape, dt=f32):
            return ctx.enter_context(nc.sbuf_tensor(name, shape, dt))

        def pb(name, shape, dt=f32):
            return ctx.enter_context(nc.psum_tensor(name, shape, dt))

        def sem(name):
            return ctx.enter_context(nc.semaphore(name))

        ident = sb("ident", [D, D])
        ones = sb("ones", [D, D])
        Wext = sb("Wext", [D, 4, WX])
        W2nat = sb("W2nat", [D, D])
        WT = sb("WT", [D, 2, D])
        A1 = sb("A1", [D, 2])
        A2 = sb("A2", [D, 8])
        A3 = sb("A3", [D, 2])
        small = sb("small", [D, 16])
        strict = sb("strict", [D, D])
        bad = sb("bad", [D, 2])
        bad_i = sb("bad_i", [D, 1], i32)
        rank1 = sb("rank1", [D, T])
        rank_i = sb("rank_i", [D, T], i32)
        keys0 = sb("keys0", [D, T])
        arena = sb("arena", [D, 50688])

        class Place:

            def __init__(self, at=0):
                self.at = at

            def take(self, *shape, dt=f32):
                n = 1
                for k in shape:
                    n *= k
                words = n if dt in (f32, i32) else n // 2
                v = arena[:, self.at:self.at + words]
                self.at += words
                assert self.at <= 50688, self.at
                if dt != f32:
                    v = v.bitcast(dt)
                if len(shape) == 2:
                    v = v.rearrange("p (a b) -> p a b", b=shape[1])
                if len(shape) == 3:
                    v = v.rearrange("p (a b c) -> p a b c", b=shape[1], c=shape[2])
                return v

        place = Place()
        X = place.take(T, D)
        AG = place.take(T, D)
        WH = place.take(T, WX)
        KB = place.take(N)
        E = place.take(N)
        A = place.take(N, dt=i32)
        PT = place.take(2, GRP * D)
        xT = PT[:, 0, 0:D]
        diag = PT[:, 1, 0:D]
        xs = PT[:, 0, D:2 * D]

        place = Place()
        REC = place.take(T, RW)
        scan_end = place.at
        ADJ = [place.take(N // 2, dt=i32) for _ in range(4)]
        SIGN = [place.take(N // 2, dt=f16) for _ in range(2)]
        FOUND = [place.take(N // 2, dt=f16) for _ in range(4)]
        col1 = place.take(CH, dt=f16)
        base = place.take(2, 64)
        top8 = place.take(2, 64)
        cand = place.take(2, 64)
        rest = place.take(2, 64)
        found = place.take(2, 64)
        top16 = place.take(2, SLOTS)
        over = place.take(2, NCH)
        deg = place.take(T)
        deg2 = place.take(2)
        NC = SLOTS + 1
        cls = place.take(NC, T)
        ind = place.take(NC, T)
        run = place.take(NC, T)
        cnt = place.take(NC)
        off = place.take(NC)
        tot = place.take(NC)
        roomy = place.take(NC)

        place = Place(scan_end)
        SX = place.take(T, 2 * D)
        IDX = place.take(T, SLOTS, dt=i32)
        IDN = place.take(T, SLOTS, dt=i32)
        PEN = place.take(T, SLOTS)
        QS = place.take(T, 4)
        RID = place.take(T, dt=i32)
        ISO = place.take(2)
        GW = 2 * SLOTS * TW
        G_AT = place.at
        NB = 4
        G = [place.take(GW) for _ in range(3)]
        G.append(place.take(GW // 2))
        AGP = [place.take(2, D) for _ in range(NB)]
        WT4 = [place.take(2 * SLOTS * 4) for _ in range(NB)]
        mx = [place.take(2 * 4) for _ in range(NB)]
        UE = [place.take(2, D) for _ in range(2)]
        st6 = place.take(2, 6)
        mv = [place.take(2, 2) for _ in range(NB)]
        ve = [place.take(2) for _ in range(NB)]
        lnv = [place.take(2) for _ in range(NB)]
        sT = [place.take(2 * D) for _ in range(2)]
        stage = [place.take(2, TW) for _ in range(2)]
        row0 = place.take(TW)
        EE = place.take(2, 4 * 2 * D)
        QB = place.take(4 * D)
        XN = arena[:, 0:T * D].rearrange("p (t d) -> p t d", d=D)
        AGL = arena[:, G_AT:G_AT + T * D].rearrange("p (b k f) -> p b k f", k=4, f=D)

        psA = pb("psA", [D, 512])
        psB = pb("psB", [D, 512])
        psT = [pb(f"psT{i}", [D, 512]) for i in range(2)]
        acc = pb("acc", [D, 512])
        psD = [pb(f"psD{i}", [D, 512]) for i in range(2)]
        psS = pb("psS", [D, 512])

        s_load = sem("setup_loads")
        s_id = sem("identity_ready")
        s_zero = sem("weights_zeroed")
        s_wt = sem("weights_transposed")
        s_wtc = sem("transposes_copied")
        s_wa = sem("score_weights_ready")
        s_setup = sem("setup_done")

        s_const = sem("constants_ready")
        s_x = sem("x_loaded")
        s_xz = sem("x_transposed")
        s_xzc = sem("xT_copied")
        s_pj = sem("x_projected")
        s_pjc = sem("projection_copied")
        s_tab0 = [sem(f"table0_written{i}") for i in range(2)]
        s_adj = [sem(f"adjacency_loaded{i}") for i in range(4)]
        s_sign = sem("signs_ready")
        s_found = sem("columns_marked")
        s_pick = sem("columns_picked")
        s_fch = sem("search_chain")
        s_cnt = sem("classes_counted")
        s_cntm = sem("counts_added")
        s_bad = sem("row_flags_ready")
        s_badm = sem("flags_added")

        f_scat = sem("records_sorted")
        f_rec = sem("records_loaded")
        f_rank = sem("rank_column_written")
        f_idx = sem("slots_ready")
        f_g = [sem(f"neighbours_gathered{i}") for i in range(NB)]
        f_gfree = sem("gather_buffer_free")
        f_e = sem("scores_ready")
        f_w = sem("weights_ready")
        f_t = sem("elu_min_ready")
        f_u = sem("elu_exp_ready")
        f_var = sem("variance_ready")
        f_ln = sem("log_ready")
        f_rs = sem("rstd_ready")
        f_x = sem("pair_normed")
        f_xT = sem("pair_transposed")
        f_xTc = sem("pair_T_copied")
        f_pr = sem("pair_projected")
        f_pc = sem("pair_projection_copied")
        f_mn = sem("mean_added")
        f_row0 = sem("mean_row_ready")
        f_tab = [sem(f"table_written{i}") for i in range(2)]
        f_tab0 = sem("mean_row_written")
        f_ch = sem("sparse_dve_chain")
        f_km = sem("kmax_steps_pe")
        f_kd = sem("kmax_steps_dve")
        f_ie = sem("isolated_scores_ready")
        f_ip = sem("isolated_probs_ready")
        f_im = sem("isolated_multiplied")
        f_agg2 = sem("layer2_sums_ready")
        f_nat = sem("layer2_scattered")
        f_natl = sem("layer2_loaded")
        f_xq = sem("layer3_rows_written")
        f_self = sem("layer3_rows_gathered")
        f_out = sem("output_rows_written")

        d_x = sem("dense_x_loaded")
        d_xs = sem("dense_x_staged")
        d_xT = sem("dense_x_transposed")
        d_xTc = sem("dense_xT_copied")
        d_pr = sem("dense_projected")
        d_wh = sem("dense_projection_copied")
        d_diag = sem("dense_diag_ready")
        d_kb = sem("dense_keys_spread")
        d_kbc = sem("dense_keys_copied")
        d_adj = sem("dense_adj_loaded")
        d_e = sem("dense_scores_ready")
        d_p = sem("dense_probs_ready")
        d_tr = sem("dense_probs_transposed")
        d_pt = sem("dense_PT_copied")
        d_mm = sem("dense_group_multiplied")
        d_out = sem("dense_tile_normed")
        d_el = sem("dense_elu_exp")
        d_bh = sem("dense_rows_regrouped")
        d_ex = sem("dense_elu_exp_ready")
        d_var = sem("dense_variance_ready")
        d_ln = sem("dense_log_ready")
        d_rs = sem("dense_rstd_ready")
        d_lay = sem("dense_layer_done")
        d_ch = sem("dense_dve_chain")
        d_store = sem("dense_out_stored")

        tables = [nc.dram_tensor(f"table{l}", (N + 1, TW), f32).ap() for l in range(4)]
        sorted_rec = nc.dram_tensor("records_in_order", (N + 1, RW), f32).ap()
        layer2_nat = nc.dram_tensor("layer2_by_node", (N, 2 * D), f32).ap()
        rows3 = nc.dram_tensor("layer3_rows", (N, TW), f32).ap()

        with nc.Block() as block:
            @block.gpsimd
            def _(pool):
                nc.gpsimd.memset(ident[:], 1.0).then_inc(s_zero, 1)
                nc.gpsimd.memset(ones[:], 1.0).then_inc(s_zero, 1)
                nc.gpsimd.memset(A2[:], 0.0).then_inc(s_zero, 1)
                nc.gpsimd.memset(Wext[:], 0.0).then_inc(s_zero, 1)
                pool.wait_ge(s_zero, 4)
                nc.gpsimd.affine_select(out=ident[:], in_=ident[:], compare_op=ALU.is_equal, fill=0.0, base=0,
                                        pattern=[[-1, D]], channel_multiplier=1).then_inc(s_id, 1)

            @block.sync
            def _(sp):
                sp.wait_ge(s_zero, 4)
                sp.dma_start(Wext[:, 0, KEY:KEY + 1], L0_attn[D:2 * D, :]).then_inc(s_load, 16)
                sp.dma_start(Wext[:, 0, QRY:QRY + 1], L0_attn[0:D, :]).then_inc(s_load, 16)
                sp.dma_start(Wext[:, 1, 0:D], L1_W).then_inc(s_load, 16)
                for k in range(2):
                    rows = slice(k * D, (k + 1) * D)
                    sp.dma_start(A1[:, k:k + 1], L1_a[rows].rearrange("(p o) -> p o", o=1)).then_inc(s_load, 16)
                    sp.dma_start(A3[:, k:k + 1], L3_a[rows, :]).then_inc(s_load, 16)
                sp.dma_start(Wext[:, 2, 0:D].rearrange("i (h d) -> i h d", h=4),
                             L2_W.rearrange("h i d -> i h d")).then_inc(s_load, 16)
                for h in range(4):
                    rows = slice(32 * h, 32 * h + 32)
                    sp.dma_start(A2[rows, h:h + 1], L2_a[h, 0:32, :]).then_inc(s_load, 16)
                    sp.dma_start(A2[rows, 4 + h:5 + h], L2_a[h, 32:64, :]).then_inc(s_load, 16)
                sp.dma_start(W2nat[:], L3_W).then_inc(s_load, 16)

            @block.tensor
            def _(pe):
                pe.wait_ge(s_id, 1)
                pe.wait_ge(s_load, 17 * 16)
                nc.tensor.transpose(psA[:, 0:D], Wext[:, 1, 0:D], ident[:])
                nc.tensor.transpose(psA[:, D:2 * D], Wext[:, 2, 0:D], ident[:])
                nc.tensor.transpose(psA[:, 2 * D:3 * D], W2nat[:], ident[:]).then_inc(s_wt, 1)
                pe.wait_ge(s_wtc, 1)
                nc.tensor.matmul(psB[:, 0:2], WT[:, 0, :], A1[:], start=True, stop=True)
                nc.tensor.matmul(psB[:, 8:16], WT[:, 1, :], A2[:], start=True, stop=True)
                nc.tensor.matmul(psB[:, 16:18], W2nat[:], A3[:], start=True, stop=True).then_inc(s_wa, 1)

            @block.vector
            def _(dve):
                dve.wait_ge(s_wt, 1)
                nc.vector.tensor_copy(WT[:, :, :], psA[:, 0:2 * D].rearrange("p (k d) -> p k d", k=2)).then_inc(s_wtc, 1)
                nc.vector.tensor_copy(Wext[:, 3, 0:D], psA[:, 2 * D:3 * D])
                nc.vector.tensor_copy(Wext[:, 0, 0:D], ident[:])
                dve.wait_ge(s_wa, 1)
                nc.vector.tensor_copy(Wext[:, 1, KEY:KEY + 1], psB[:, 0:1])
                nc.vector.tensor_copy(Wext[:, 1, QRY:QRY + 1], psB[:, 1:2])
                nc.vector.tensor_copy(Wext[:, 2, KEY:KEY + 8], psB[:, 8:16])
                nc.vector.tensor_copy(Wext[:, 3, QRY:QRY + 1], psB[:, 16:17])
                nc.vector.tensor_copy(Wext[:, 3, KEY:KEY + 1], psB[:, 17:18]).then_inc(s_setup, 1)
                dve.wait_ge(s_setup, 1)

        passes = [(l, h) for l, (heads, _, _) in enumerate(LAYERS) for h in range(heads)]
        GROUPS = T // GRP
        HEADS_END = sum(heads for heads, _, _ in LAYERS[:3]) - 1
        by_head = nc.dram_tensor("sums_by_head", (4, N, D // 4), f32).ap()
        LAY_LINKS = [0, 6, 0, 1]

        def dense_sync(sp):
            sp.dma_start(X[:], x.rearrange("(t p) d -> p t d", p=D)).then_inc(d_x, 16)
            for n in range(len(passes)):
                if n:
                    sp.wait_ge(d_e, n * T)
                sp.dma_start(A[:], adj[0:D, :]).then_inc(d_adj, 16)
                with sp.Fori(1, T) as t:
                    sp.wait_ge(d_e, t + n * T)
                    sp.dma_start(A[:], adj.rearrange("(t p) j -> t p j", p=D)[bass.ds(t, 1), :, :].rearrange("o p j -> p (o j)")).then_inc(d_adj, 16)
                if n == HEADS_END:
                    sp.wait_ge(d_out, (n + 1) * T)
                    heads = LAYERS[2][0]
                    for h in range(heads):
                        sp.dma_start(by_head.rearrange("h (t p) d -> h p t d", p=D)[h],
                                     AG[:, :, h * (D // heads):(h + 1) * (D // heads)]).then_inc(d_bh, 16)
                    sp.wait_ge(d_bh, 16 * heads)
                    sp.dma_start(AG[:], by_head.rearrange("h (m k) d -> (h m) (k d)", k=heads)
                                 .rearrange("(t p) f -> p t f", p=D)).then_inc(d_bh, 16)
            sp.wait_ge(d_lay, len(LAYERS))
            sp.dma_start(out.rearrange("(t p) d -> p t d", p=D), X[:]).then_inc(d_store, 16)
            sp.wait_ge(d_store, 16)

        def dense_tensor(pe):
            n = 0
            for l, (heads, _, _) in enumerate(LAYERS):
                with pe.Fori(0, T) as t:
                    pe.wait_ge(d_xs, t + (l * T + 1))
                    nc.tensor.transpose(psA[:, 0:D], xs, ident[:]).then_inc(d_xT, 1)
                    pe.wait_ge(d_xTc, t + (l * T + 1))
                    nc.tensor.matmul(psB[:, 0:WX], xT, Wext[:, l, :], start=True, stop=True).then_inc(d_pr, 1)
                    pe.wait_ge(d_wh, t + (l * T + 1))
                for h in range(heads):
                    dh = D // heads
                    with pe.Fori(0, T) as t:
                        pe.wait_ge(d_diag, t + (n * T + 1))
                        nc.tensor.matmul(psA[:, 0:D], ones[:], diag, start=True, stop=True).then_inc(d_kb, 1)
                        pe.wait_ge(d_kbc, t + (n * T + 1))
                    with pe.Fori(0, T) as t:
                        pe.wait_ge(d_p, t + (n * T + 1))
                        if n:
                            pe.wait_ge(d_out, t + n * T)
                        else:
                            pe.wait_ge(d_kbc, T)
                        for g in range(GROUPS):
                            for j in range(g * GRP, (g + 1) * GRP):
                                last = nc.tensor.transpose(psT[g % 2][:, j % GRP * D:(j % GRP + 1) * D],
                                                           E[:, j * D:(j + 1) * D], ident[:])
                            last.then_inc(d_tr, 1)
                            pe.wait_ge(d_pt, t * GROUPS + (n * T * GROUPS + g + 1))
                            for j in range(g * GRP, (g + 1) * GRP):
                                last = nc.tensor.matmul(acc[:, 0:dh], PT[:, g % 2, j % GRP * D:(j % GRP + 1) * D],
                                                        WH[:, j, h * dh:(h + 1) * dh],
                                                        start=(j == 0), stop=(j == T - 1))
                            last.then_inc(d_mm, 1)
                    n += 1

        def dense_scalar(act):
            n = 0
            for l, (heads, _, _) in enumerate(LAYERS):
                if l:
                    act.wait_ge(d_lay, l)
                else:
                    act.wait_ge(d_x, 16)
                with act.Fori(0, T) as t:
                    nc.scalar.copy(xs, X[:, bass.ds(t, 1), :].rearrange("p o d -> p (o d)")).then_inc(d_xs, 1)
                    act.wait_ge(d_xT, t + (l * T + 1))
                    nc.scalar.copy(xT, psA[:, 0:D]).then_inc(d_xTc, 1)
                    act.wait_ge(d_pr, t + (l * T + 1))
                    nc.scalar.copy(WH[:, bass.ds(t, 1), :].rearrange("p o d -> p (o d)"), psB[:, 0:WX]).then_inc(d_wh, 1)
                for h in range(heads):
                    with act.Fori(0, T) as t:
                        act.wait_ge(d_kb, t + (n * T + 1))
                        nc.scalar.copy(KB[:, bass.ds(t * D, D)], psA[:, 0:D]).then_inc(d_kbc, 1)
                    with act.Fori(0, T) as t:
                        act.wait_ge(d_e, t + (n * T + 1))
                        nc.scalar.activation(E[:], E[:], ACT.Exp, bias=small[:, 1:2], accum_out=small[:, 2:3]).then_inc(d_p, 1)
                        with act.Fori(0, GROUPS // 2) as g:
                            for b in range(2):
                                at = t * GROUPS + g * 2 + (n * T * GROUPS + b)
                                act.wait_ge(d_tr, at + 1)
                                nc.scalar.copy(PT[:, b, :], psT[b][:]).then_inc(d_pt, 1)
                    n += 1
                with act.Fori(0, T) as t:
                    if l == 1:
                        act.wait_ge(d_el, t + 1)
                        nc.scalar.activation(E[:, 0:D], E[:, 0:D], ACT.Exp).then_inc(d_ex, 1)
                    act.wait_ge(d_var, t + (l * T + 1))
                    nc.scalar.activation(small[:, 9:10], small[:, 8:9], ACT.Ln).then_inc(d_ln, 1)
                    act.wait_ge(d_ln, t + (l * T + 1))
                    nc.scalar.activation(small[:, 8:9], small[:, 9:10], ACT.Exp, scale=-0.5).then_inc(d_rs, 1)

        def dense_vector(dve):
            ch = Chain(dve, d_ch)
            n = 0
            for l, (heads, slope, neg) in enumerate(LAYERS):
                dve.wait_ge(d_wh, (l + 1) * T)
                for h in range(heads):
                    dh = D // heads
                    with dve.Fori(0, T) as t:
                        if n:
                            dve.wait_ge(d_kbc, t + n * T)
                            dve.wait_ge(d_mm, n * T * GROUPS)
                        else:
                            dve.wait_ge(d_xTc, T)
                        nc.vector.tensor_scalar(diag, ident[:], WH[:, bass.ds(t, 1), KEY + h:KEY + h + 1].rearrange("p o d -> p (o d)"),
                                                None, ALU.mult).then_inc(d_diag, 1)
                        dve.wait_ge(d_kb, t + (n * T + 1))
                    dve.wait_ge(d_kbc, (n + 1) * T)
                    with dve.Fori(0, T) as t:
                        ch.loop(t, 9 if l else 8)
                        ch.link(nc.vector.tensor_scalar(E[:], KB[:], WH[:, bass.ds(t, 1), QRY + h:QRY + h + 1].rearrange("p o d -> p (o d)"),
                                                        None, ALU.add))
                        ch.link(nc.vector.scalar_tensor_tensor(out=E[:], in0=E[:], scalar=slope, in1=E[:], op0=ALU.mult, op1=ALU.max))
                        dve.wait_ge(d_adj, t * 16 + (n * T + 1) * 16)
                        M = A[:].bitcast(f32)
                        ch.link(nc.vector.tensor_scalar(M, A[:], 0.0, None, ALU.is_gt))
                        if l:
                            ch.link(nc.vector.tensor_tensor(E[:], E[:], M, ALU.mult))
                        ch.link(nc.vector.tensor_scalar(M, M, 1.0, -neg, ALU.subtract, ALU.mult))
                        ch.link(nc.vector.tensor_tensor(E[:], E[:], M, ALU.add))
                        ch.link(nc.vector.reduce_max(small[:, 0:1], E[:], AX.X))
                        nc.vector.tensor_scalar(small[:, 1:2], small[:, 0:1], -1.0, None, ALU.mult).then_inc(d_e, 1)
                        dve.wait_ge(d_mm, t * GROUPS + (n * T + 1) * GROUPS)
                        ch.link(nc.vector.reciprocal(small[:, 3:4], small[:, 2:3]))
                        ch.link(nc.vector.tensor_scalar(AG[:, bass.ds(t, 1), h * dh:(h + 1) * dh].rearrange("p o d -> p (o d)"),
                                                        acc[:, 0:dh], small[:, 3:4], None, ALU.mult))
                        nc.vector.tensor_copy(small[:, 4:5], small[:, 3:4]).then_inc(d_out, 1)
                        ch.endloop(T)
                    n += 1
                if l == 2:
                    dve.wait_ge(d_bh, 16 * (heads + 1))
                with dve.Fori(0, T) as t:
                    ag = AG[:, bass.ds(t, 1), :].rearrange("p o d -> p (o d)")
                    xt = X[:, bass.ds(t, 1), :].rearrange("p o d -> p (o d)")
                    ch.loop(t, {0: 0, 1: 3, 2: 0, 3: 1}[l] + 7)
                    if l == 1:
                        nc.vector.tensor_scalar(E[:, 0:D], ag, 0.0, None, ALU.min).then_inc(d_el, 1)
                        ch.link(nc.vector.tensor_scalar(ag, ag, 0.0, None, ALU.max))
                        dve.wait_ge(d_ex, t + 1)
                        ch.link(nc.vector.tensor_scalar(E[:, 0:D], E[:, 0:D], 1.0, None, ALU.subtract))
                        ch.link(nc.vector.tensor_tensor(ag, ag, E[:, 0:D], ALU.add))
                    if l == 3:
                        ch.link(nc.vector.tensor_scalar(ag, ag, 0.0, None, ALU.max))
                    xw = E[:, D:2 * D]
                    ch.link(nc.vector.tensor_tensor(xw, xt, ag, ALU.add))
                    ch.link(nc.vector.reduce_sum(small[:, 6:7], xw, AX.X))
                    ch.link(nc.vector.tensor_scalar(small[:, 6:7], small[:, 6:7], 1.0 / D, None, ALU.mult))
                    ch.link(nc.vector.tensor_scalar(xw, xw, small[:, 6:7], None, ALU.subtract))
                    ch.link(nc.vector.tensor_tensor(E[:, 0:D], xw, xw, ALU.mult))
                    ch.link(nc.vector.reduce_sum(small[:, 7:8], E[:, 0:D], AX.X))
                    nc.vector.tensor_scalar(small[:, 8:9], small[:, 7:8], 1.0 / D, EPS, ALU.mult, ALU.add).then_inc(d_var, 1)
                    dve.wait_ge(d_rs, t + (l * T + 1))
                    ch.link(nc.vector.tensor_scalar(xt, xw, small[:, 8:9], None, ALU.mult))
                    ch.endloop(T)
                nc.vector.tensor_copy(small[:, 10:11], small[:, 8:9]).then_inc(d_lay, 1)

        STEPS = T // 2
        adj_units = adj.rearrange("(i t p) (h c) -> i t h p c", t=2, p=D, h=2)

        def unit(i, u):
            return adj_units[bass.ds(i, 1), u // 2, u % 2, :, :].rearrange("o p c -> p (o c)")

        with nc.Block() as block:
            @block.gpsimd
            def _(pool):
                nc.gpsimd.iota(col1, [[1, CH]], base=1, channel_multiplier=0,
                               allow_small_or_imprecise_dtypes=True).then_inc(s_const, 1)
                nc.gpsimd.iota(base, [[0, 2], [CH, NCH], [0, 8]], base=0, channel_multiplier=0,
                               allow_small_or_imprecise_dtypes=True).then_inc(s_const, 1)
                nc.gpsimd.iota(cls, [[-1, NC], [0, T]], base=SLOTS, channel_multiplier=0,
                               allow_small_or_imprecise_dtypes=True).then_inc(s_const, 1)
                for c in range(NC):
                    room = 2 * D * sum(r >= SLOTS - c for r in ROOM) if c < SLOTS else N
                    nc.gpsimd.memset(roomy[:, c:c + 1], float(room)).then_inc(s_const, 1)
                nc.gpsimd.memset(strict[:], 1.0).then_inc(s_const, 1)
                nc.gpsimd.memset(over, 0.0).then_inc(s_const, 1)
                pool.wait_ge(s_const, NC + 5)
                nc.gpsimd.affine_select(out=strict[:], in_=strict[:], compare_op=ALU.is_gt, fill=0.0, base=0,
                                        pattern=[[1, D]], channel_multiplier=-1).then_inc(s_const, 1)
                pool.wait_ge(s_x, 16)
                nc.gpsimd.memset(REC[:, :, R_ONE:R_ONE + 1], 1.0).then_inc(s_const, 1)
                nc.gpsimd.memset(REC[:, :, R_ID + 1:RW], 0.0).then_inc(s_const, 1)
                nc.gpsimd.iota(REC[:, :, R_ID:R_ID + 1], [[D, T], [0, 1]], base=0, channel_multiplier=1,
                               allow_small_or_imprecise_dtypes=True).then_inc(s_const, 1)
                pool.wait_ge(s_const, NC + 9)

            @block.sync
            def _(sp):
                sp.dma_start(REC[:, :, 0:D], x.rearrange("(t p) d -> p t d", p=D)).then_inc(s_x, 16)
                for u in range(4):
                    sp.dma_start(ADJ[u], unit(0, u)).then_inc(s_adj[u], 16)
                for p in range(PAIRS):
                    sp.wait_ge(s_pjc, p + 1)
                    sp.dma_start(tables[0][1 + 2 * p * D:1 + 2 * (p + 1) * D, :].rearrange("(t p) w -> p t w", p=D),
                                 stage[p % 2]).then_inc(s_tab0[p % 2], 16)
                with sp.Fori(1, STEPS) as i:
                    for u in range(4):
                        sp.wait_ge(s_sign, i * 4 + (u - 3))
                        sp.dma_start(ADJ[u], unit(i, u)).then_inc(s_adj[u], 16)
                sp.wait_ge(s_tab0[0], 16 * PAIRS // 2)
                sp.wait_ge(s_tab0[1], 16 * PAIRS // 2)

            @block.scalar
            def _(act):
                nc.scalar.preload_act_table_set("natural_log_exp_and_others")
                for p in range(PAIRS):
                    act.wait_ge(s_xz, p + 1)
                    nc.scalar.copy(sT[p % 2], psT[p % 2][:, 0:2 * D]).then_inc(s_xzc, 1)
                    act.wait_ge(s_pj, p + 1)
                    if p >= 2:
                        act.wait_ge(s_tab0[p % 2], 16 * (p // 2))
                    prj = [psA, psB][p % 2][:, 0:2 * WX].rearrange("p (t w) -> p t w", t=2)
                    nc.scalar.copy(keys0[:, 2 * p:2 * p + 2], prj[:, :, KEY])
                    nc.scalar.copy(REC[:, 2 * p:2 * p + 2, R_QRY], prj[:, :, QRY])
                    nc.scalar.copy(stage[p % 2], prj[:, :, 0:TW]).then_inc(s_pjc, 1)
                with act.Fori(0, STEPS) as i:
                    for u in range(4):
                        act.wait_ge(s_adj[u], i * 16 + 16)
                        act.wait_ge(s_found, i * 4 + (u + 1))
                        nc.scalar.activation(SIGN[u % 2], ADJ[u], ACT.Sign).then_inc(s_sign, 1)

            @block.tensor
            def _(pe):
                pe.wait_ge(s_x, 16)
                for p in range(PAIRS):
                    if p >= 2:
                        pe.wait_ge(s_pjc, p - 1)
                    for t in range(2):
                        last = nc.tensor.transpose(psT[p % 2][:, t * D:(t + 1) * D], REC[:, 2 * p + t, 0:D], ident[:])
                    last.then_inc(s_xz, 1)
                    pe.wait_ge(s_xzc, p + 1)
                    for t in range(2):
                        last = nc.tensor.matmul([psA, psB][p % 2][:, t * WX:(t + 1) * WX], sT[p % 2][:, t * D:(t + 1) * D],
                                                Wext[:, 0, :], start=True, stop=True)
                    last.then_inc(s_pj, 1)
                pe.wait_ge(s_const, NC + 9)
                pe.wait_ge(s_cnt, 1)
                nc.tensor.matmul(psS[:, 0:NC], strict[:], cnt, start=True, stop=True)
                nc.tensor.matmul(psS[:, 32:32 + NC], ones[:], cnt, start=True, stop=True).then_inc(s_cntm, 1)
                pe.wait_ge(s_bad, 1)
                nc.tensor.matmul(psS[:, 64:65], ones[:], bad[:, 0:1], start=True, stop=True).then_inc(s_badm, 1)

            @block.vector
            def _(dve):
                ch = Chain(dve, s_fch)
                dve.wait_ge(s_const, NC + 5)
                nc.vector.memset(small[:, 0:1], 0.0).then_inc(s_found, 1)
                nc.vector.memset(small[:, 1:2], 0.0).then_inc(s_found, 1)
                for k in range(4):
                    nc.vector.memset(small[:, 2 + k:3 + k], 0.0).then_inc(s_pick, 1)
                cols = col1.unsqueeze(1).broadcast_to([D, N // 2 // CH, CH])

                def mark(n, u):
                    dve.wait_ge(s_found, n + 2)
                    dve.wait_ge(s_sign, n + 1)
                    dve.wait_ge(s_pick, n + 1)
                    nc.vector.tensor_tensor(FOUND[u % 4].rearrange("p (c k) -> p c k", k=CH),
                                            SIGN[u % 2].rearrange("p (c k) -> p c k", k=CH), cols, ALU.mult).then_inc(s_found, 1)

                def pick(n, u):
                    half = top8[:, u // 2, (u % 2) * 32:(u % 2) * 32 + 32]
                    for c in range(N // 2 // CH):
                        last = nc.vector.max(half[:, 8 * c:8 * c + 8], FOUND[u % 4][:, c * CH:(c + 1) * CH])
                    last.then_inc(s_pick, 1)

                def gather_step(i, ds):
                    ch.link(nc.vector.tensor_tensor(cand, top8, base, ALU.add))
                    ch.link(nc.vector.scalar_tensor_tensor(out=cand, in0=top8, scalar=0.0, in1=cand, op0=ALU.is_gt, op1=ALU.mult))
                    ch.add(nc.vector.tensor_scalar(found, cand, 0.0, None, ALU.is_gt))
                    for t in range(2):
                        ch.add(nc.vector.max(top16[:, t, 0:8], cand[:, t, :]))
                    ch.wait()
                    ch.add(nc.vector.reduce_sum(deg2, found, AX.X))
                    for t in range(2):
                        ch.add(nc.vector.match_replace(rest[:, t, :], top16[:, t, 0:8], cand[:, t, :], 0.0))
                    ch.wait()
                    full = top8.rearrange("p t (c k) -> p t c k", k=8)[:, :, :, 7]
                    ch.add(nc.vector.tensor_tensor(over, over, full, ALU.max))
                    for t in range(2):
                        ch.add(nc.vector.max(top16[:, t, 8:16], rest[:, t, :]))
                    ch.add(nc.vector.tensor_copy(deg[:, ds], deg2))
                    ch.wait()
                    ch.link(nc.vector.tensor_copy(REC[:, ds, R_SLOT:R_SLOT + SLOTS], top16))

                PER = 13
                mark(0, 0)
                with dve.Fori(0, STEPS - 1) as i:
                    ch.loop(i, PER)
                    for u in range(4):
                        mark(i * 4 + (u + 1), u + 1)
                        pick(i * 4 + u, u)
                    dve.wait_ge(s_pick, i * 4 + 8)
                    gather_step(i, bass.ds(i * 2, 2))
                    ch.endloop(STEPS - 1)
                end = 4 * (STEPS - 1)
                for u in range(4):
                    if u < 3:
                        mark(end + u + 1, u + 1)
                    else:
                        dve.wait_ge(s_found, end + u + 3)
                    pick(end + u, u)
                dve.wait_ge(s_pick, end + 8)
                gather_step(STEPS - 1, slice(T - 2, T))

                ch.link(nc.vector.tensor_scalar(run[:, 0, :], deg, float(SLOTS), None, ALU.min))
                ch.link(nc.vector.tensor_tensor(ind, cls, run[:, 0:1, :].broadcast_to([D, NC, T]), ALU.is_equal))
                flat = "p c t -> p (c t)"
                ch.link(nc.vector.tensor_tensor_scan(run.rearrange(flat), ind.rearrange(flat), ind.rearrange(flat), 0.0, ALU.add, ALU.max))
                nc.vector.reduce_sum(cnt, ind, AX.X).then_inc(s_cnt, 1)
                dve.wait_ge(s_cntm, 1)
                ch.link(nc.vector.tensor_copy(tot, psS[:, 32:32 + NC]))
                ch.link(nc.vector.tensor_tensor_scan(off, tot, tot, 0.0, ALU.add, ALU.max))
                ch.link(nc.vector.tensor_tensor(cls[:, 0, 0:NC], off, roomy, ALU.is_gt))
                ch.link(nc.vector.tensor_copy(cls[:, 1, 0:1], off[:, SLOTS - 1:SLOTS]))
                ch.link(nc.vector.tensor_tensor(off, off, tot, ALU.subtract))
                ch.link(nc.vector.tensor_tensor(off, off, psS[:, 0:NC], ALU.add))
                ch.link(nc.vector.tensor_tensor(off, off, run[:, :, T - 1], ALU.subtract))
                ch.link(nc.vector.tensor_tensor(off, off, cnt, ALU.add))
                ch.link(nc.vector.tensor_tensor(run, run, off.unsqueeze(2).broadcast_to([D, NC, T]), ALU.add))
                ch.link(nc.vector.tensor_tensor(run, run, ind, ALU.mult))
                ch.link(nc.vector.reduce_sum(rank1[:], run.rearrange("p c t -> p t c"), AX.X))
                ch.link(nc.vector.tensor_copy(rank_i[:], rank1[:]))

                ch.link(nc.vector.reduce_max(small[:, 0:1], cls[:, 0, 0:NC], AX.X))
                ch.link(nc.vector.tensor_reduce(small[:, 1:2], over, AX.XY, ALU.max))
                ch.link(nc.vector.reduce_max(small[:, 2:3], deg, AX.X))
                ch.link(nc.vector.tensor_scalar(small[:, 2:3], small[:, 2:3], SLOTS + 0.5, None, ALU.is_gt))
                ch.link(nc.vector.tensor_scalar(small[:, 3:4], cls[:, 1, 0:1], N - 2 * D - 0.5, None, ALU.is_lt))
                ch.link(nc.vector.reduce_max(small[:, 4:5], small[:, 0:4], AX.X))
                nc.vector.tensor_scalar(bad[:, 0:1], small[:, 4:5], 0.0, 1.0 / D, ALU.is_gt, ALU.mult).then_inc(s_bad, 1)
                dve.wait_ge(s_badm, 1)
                if FORCE == "dense":
                    ch.link(nc.vector.memset(bad_i[:], 1))
                else:
                    ch.link(nc.vector.tensor_scalar(bad_i[:], psS[:, 64:65], 0.0, None, ALU.is_gt))

        def buf(n, p):
            S = ROOM[p]
            return G[n % NB][:, 0:2 * S * TW].rearrange("p (t s w) -> p t s w", t=2, w=TW)

        def wts(n, p, heads):
            S = ROOM[p]
            return WT4[n % NB][:, 0:2 * S * heads].rearrange("p (t s h) -> p t s h", t=2, h=heads)

        total_g = [0] * NB
        reach = {}
        for n in range(4 * PAIRS):
            total_g[n % NB] += 2 * ROOM[n % PAIRS] * 16
            reach[n] = total_g[n % NB]

        def fast_gpsimd(pool):
            for t in range(T):
                pool.indirect_dma_start(sorted_rec, bass.IndirectOffsetOnAxis(ap=rank_i[:, t:t + 1], axis=0),
                                        REC[:, t, :], None).then_inc(f_scat, 16)

            def gather(l, p):
                n = l * PAIRS + p
                if n >= NB:
                    pool.wait_ge(f_gfree, n - NB + 1)
                dst = buf(n, p)
                for t in range(2):
                    for k in range(ROOM[p]):
                        pool.indirect_dma_start(dst[:, t, k, :], None, tables[l],
                                                bass.IndirectOffsetOnAxis(ap=(IDN if l in (0, 3) else IDX)[:, 2 * p + t, k:k + 1], axis=0)).then_inc(f_g[n % NB], 16)

            pool.wait_ge(f_idx, 2)
            pool.wait_ge(f_rank, 32)
            for p in range(PAIRS):
                gather(0, p)
            for l in (1, 2):
                pool.wait_ge(f_tab[0], 16 * l * PAIRS // 2)
                pool.wait_ge(f_tab[1], 16 * l * PAIRS // 2)
                pool.wait_ge(f_tab0, 16 * l)
                for p in range(PAIRS):
                    gather(l, p)
            for p in range(PAIRS):
                pool.wait_ge(f_agg2, p + 1)
                for t in range(2 * p, 2 * p + 2):
                    pool.indirect_dma_start(layer2_nat, bass.IndirectOffsetOnAxis(ap=RID[:, t:t + 1], axis=0),
                                            SX[:, t, :], None).then_inc(f_nat, 16)
            pool.wait_ge(f_xq, 16 * (PAIRS + 1))
            for t in range(T):
                pool.indirect_dma_start(SX[:, t, 0:TW], None, rows3,
                                        bass.IndirectOffsetOnAxis(ap=RID[:, t:t + 1], axis=0)).then_inc(f_self, 16)
            pool.wait_ge(f_tab[0], 16 * 3 * PAIRS // 2)
            pool.wait_ge(f_tab[1], 16 * 3 * PAIRS // 2)
            pool.wait_ge(f_tab0, 16 * 3)
            for p in range(PAIRS):
                gather(3, p)
                if p >= 4:
                    store(pool, p - 4)
            for p in range(PAIRS - 4, PAIRS):
                store(pool, p)
            pool.wait_ge(f_out, 16 * T)

        def store(pool, p):
            pool.wait_ge(f_x, 2 * PAIRS + PAIRS + p + 1)
            for t in range(2 * p, 2 * p + 2):
                pool.indirect_dma_start(out, bass.IndirectOffsetOnAxis(ap=RID[:, t:t + 1], axis=0),
                                        SX[:, t, 0:D], None).then_inc(f_out, 16)

        def table_rows(l, p):
            return tables[l][1 + 2 * p * D:1 + 2 * (p + 1) * D, :].rearrange("(t p) w -> p t w", p=D)

        def fast_sync(sp):
            with nc.allow_non_contiguous_dma(reason="one column"):
                sp.dma_start(tables[0][1:N + 1, KEY + 1:KEY + 2].rearrange("(t p) w -> p t w", p=D),
                             rank1[:].unsqueeze(2)).then_inc(f_rank, 16)
            sp.wait_ge(f_row0, 1)
            sp.dma_start(tables[0][0:1, :], row0[0:1, :]).then_inc(f_rank, 16)
            sp.wait_ge(f_scat, 16 * T)
            sp.dma_start(SX[:, :, 0:RW], sorted_rec[1:N + 1, :].rearrange("(t p) w -> p t w", p=D)).then_inc(f_rec, 16)
            for l in (1, 2, 3):
                if l == 3:
                    sp.wait_ge(f_nat, 16 * T)
                    sp.dma_start(XN, layer2_nat[:, 0:D].rearrange("(t p) d -> p t d", p=D)).then_inc(f_natl, 16)
                    for k in range(4):
                        sp.dma_start(AGL[:, :, k, :], layer2_nat.rearrange("(b p k) w -> k p b w", p=D, k=4)[k, :, :, D:2 * D]).then_inc(f_natl, 16)
                for p in range(PAIRS):
                    sp.wait_ge(f_pc, (l - 1) * PAIRS + p + 1)
                    sp.dma_start(table_rows(l, p), stage[p % 2]).then_inc(f_tab[p % 2], 16)
                    if l == 3:
                        sp.dma_start(rows3[2 * p * D:2 * (p + 1) * D, 0:D].rearrange("(t p) w -> p t w", p=D),
                                     XN[:, 2 * p:2 * p + 2, :]).then_inc(f_xq, 16)
                sp.wait_ge(f_row0, l + 1)
                sp.dma_start(tables[l][0:1, :], row0[0:1, :]).then_inc(f_tab0, 16)
                if l == 3:
                    sp.dma_start(rows3[:, D:TW].rearrange("(t p) w -> p t w", p=D), QS).then_inc(f_xq, 16)

        def fast_scalar(act):
            def iso(c):
                act.wait_ge(f_ie, c + 1)
                if c >= 2:
                    act.wait_ge(f_im, c - 1)
                nc.scalar.activation(EE[:, c % 2, :], EE[:, c % 2, :], ACT.Exp).then_inc(f_ip, 1)

            def exp_w(l, p):
                n = l * PAIRS + p
                act.wait_ge(f_e, n + 1)
                w = WT4[n % NB][:, 0:2 * ROOM[p] * LAYERS[l][0]]
                nc.scalar.activation(w, w, ACT.Exp).then_inc(f_w, 1)

            def elu(p):
                act.wait_ge(f_t, p + 1)
                nc.scalar.activation(UE[p % 2], UE[p % 2], ACT.Exp).then_inc(f_u, 1)

            def rstd(m, p):
                act.wait_ge(f_var, m + 1)
                nc.scalar.activation(lnv[m % NB], ve[m % NB], ACT.Ln).then_inc(f_ln, 1)
                act.wait_ge(f_ln, m + 1)
                nc.scalar.activation(ve[m % NB], lnv[m % NB], ACT.Exp, scale=-0.5).then_inc(f_rs, 1)

            def project(l, p):
                n = (l - 1) * PAIRS + p
                act.wait_ge(f_xT, n + 1)
                nc.scalar.copy(sT[p % 2], psT[p % 2][:, 0:2 * D]).then_inc(f_xTc, 1)
                act.wait_ge(f_pr, n + 1)
                if n >= 2:
                    act.wait_ge(f_tab[p % 2], 16 * (n // 2))
                    act.wait_ge(f_mn, n - 1)
                prj = [psA, psB][p % 2][:, 0:2 * WX].rearrange("p (t w) -> p t w", t=2)
                nc.scalar.copy(QS[:, 2 * p:2 * p + 2, :], prj[:, :, QRY:WX])
                nc.scalar.copy(stage[p % 2], prj[:, :, 0:TW]).then_inc(f_pc, 1)

            def mean(l):
                act.wait_ge(f_mn, l * PAIRS)
                if l > 1:
                    act.wait_ge(f_tab0, 16 * (l - 1))
                nc.scalar.activation(row0[0:1, :], acc[0:1, 0:TW], ACT.Copy, scale=1.0 / N).then_inc(f_row0, 1)

            for l in range(4):
                for q in range(PAIRS + 4):
                    if l == 0 and 4 <= q < 20:
                        iso(q - 4)
                    if q < PAIRS:
                        exp_w(l, q)
                    if l == 1 and 1 <= q <= PAIRS:
                        elu(q - 1)
                    if l != 2 and 2 <= q < PAIRS + 2:
                        rstd(l * PAIRS + q - 2, q - 2)
                    if l < 2 and 4 <= q:
                        project(l + 1, q - 4)
                if l < 2:
                    mean(l + 1)
                if l == 2:
                    for p in range(PAIRS + 2):
                        if p < PAIRS:
                            rstd(2 * PAIRS + p, p)
                        if p >= 2:
                            project(3, p - 2)
                    mean(3)

        def fast_tensor(pe):
            pe.wait_ge(f_kd, 1)
            nc.tensor.matmul(psS[0:1, 0:D], small[:, 0:1], ident[:], start=True, stop=True).then_inc(f_km, 1)
            pe.wait_ge(f_kd, 2)
            nc.tensor.matmul(psS[:, D:D + 1], ones[0:1, :], small[0:1, 1:2], start=True, stop=True).then_inc(f_km, 1)
            for k in range(4):
                pe.wait_ge(f_kd, 3 + k)
                nc.tensor.matmul(psS[:, k * D:(k + 1) * D], ones[:], EE[:, 0, k * D:(k + 1) * D],
                                 start=True, stop=True).then_inc(f_km, 1)

            def iso(c):
                pe.wait_ge(f_ip, c + 1)
                for j in range(4 * c, 4 * c + 4):
                    for t in range(2):
                        e = EE[:, c % 2, (j % 4) * 2 * D + t * D:(j % 4) * 2 * D + (t + 1) * D]
                        last = nc.tensor.matmul(psD[t][:, 0:D + 1], e, REC[:, j, 0:D + 1], start=(j == 0), stop=(j == T - 1))
                last.then_inc(f_im, 1)

            def project(l, p):
                n = (l - 1) * PAIRS + p
                pe.wait_ge(f_x, n + 1)
                if n >= 2:
                    pe.wait_ge(f_pc, n - 1)
                for t in range(2):
                    src = XN[:, 2 * p + t, :] if l == 3 else SX[:, 2 * p + t, 0:D]
                    last = nc.tensor.transpose(psT[p % 2][:, t * D:(t + 1) * D], src, ident[:])
                last.then_inc(f_xT, 1)
                pe.wait_ge(f_xTc, n + 1)
                for t in range(2):
                    last = nc.tensor.matmul([psA, psB][p % 2][:, t * WX:(t + 1) * WX], sT[p % 2][:, t * D:(t + 1) * D],
                                            Wext[:, l, :], start=True, stop=True)
                last.then_inc(f_pr, 1)
                if n >= 1 and p >= 1:
                    average(l, p - 1)
                if p == PAIRS - 1:
                    average(l, p)

            def average(l, p):
                n = (l - 1) * PAIRS + p
                pe.wait_ge(f_pc, n + 1)
                if p == 0 and l > 1:
                    pe.wait_ge(f_row0, l)
                for t in range(2):
                    last = nc.tensor.matmul(acc[0:1, 0:TW], ones[:, 0:1], stage[p % 2][:, t, :],
                                            start=(p == 0 and t == 0), stop=(p == PAIRS - 1 and t == 1))
                last.then_inc(f_mn, 1)

            for l in (1, 2, 3):
                for p in range(PAIRS):
                    if l == 1 and p < T // 4:
                        iso(p)
                    project(l, p)

        def fast_vector(dve):
            ch = Chain(dve, f_ch)
            nc.vector.memset(row0[:], 0.0).then_inc(f_row0, 1)
            dve.wait_ge(f_rec, 16)
            slots = SX[:, :, R_SLOT:R_SLOT + SLOTS]
            nc.vector.tensor_copy(IDX, slots).then_inc(f_idx, 1)
            nc.vector.tensor_copy(IDN, slots).then_inc(f_idx, 1)
            ch.link(nc.vector.tensor_scalar(PEN, slots, 0.0, None, ALU.is_gt))
            ch.link(nc.vector.tensor_scalar(PEN, PEN, 1.0, BIG, ALU.subtract, ALU.mult))
            ch.link(nc.vector.memset(PEN[:, :, 0:1], 0.0))
            ch.link(nc.vector.tensor_copy(QS[:, :, 0], SX[:, :, R_QRY]))
            ch.link(nc.vector.tensor_copy(RID, SX[:, :, R_ID]))
            ch.link(nc.vector.tensor_scalar(ISO, SX[:, T - 2:T, R_SLOT], 0.0, None, ALU.is_equal))
            nc.vector.reduce_max(small[:, 0:1], keys0[:], AX.X).then_inc(f_kd, 1)
            dve.wait_ge(f_km, 1)
            nc.vector.reduce_max(small[0:1, 1:2], psS[0:1, 0:D], AX.X).then_inc(f_kd, 1)
            dve.wait_ge(f_km, 2)
            slope, neg = LAYERS[0][1], LAYERS[0][2]
            ch.link(nc.vector.tensor_copy(small[:, 2:3], psS[:, D:D + 1]))
            ch.link(nc.vector.tensor_scalar(small[:, 4:6], QS[:, T - 2:T, 0], small[:, 2:3], None, ALU.add))
            ch.link(nc.vector.scalar_tensor_tensor(out=small[:, 4:6], in0=small[:, 4:6], scalar=slope, in1=small[:, 4:6],
                                                   op0=ALU.mult, op1=ALU.max))
            ch.link(nc.vector.tensor_scalar(small[:, 4:6], small[:, 4:6], neg, None, ALU.add))
            for k in range(4):
                v = QS[:, T - 2 + k, 0:1] if k < 2 else small[:, 2 + k:3 + k]
                nc.vector.tensor_scalar(EE[:, 0, k * D:(k + 1) * D], ident[:], v, None, ALU.mult).then_inc(f_kd, 1)
            dve.wait_ge(f_km, 6)
            ch.link(nc.vector.tensor_copy(QB, psS[:]))

            def iso(c):
                if c >= 2:
                    dve.wait_ge(f_im, c - 1)
                e = EE[:, c % 2, :]
                e3 = e.rearrange("p (j i) -> p j i", j=4)
                ch.link(nc.vector.tensor_tensor(e3, QB[:, 0:2 * D].unsqueeze(1).broadcast_to([D, 4, 2 * D]),
                                                keys0[:, 4 * c:4 * c + 4].unsqueeze(2).broadcast_to([D, 4, 2 * D]), ALU.add))
                ch.link(nc.vector.scalar_tensor_tensor(out=e, in0=e, scalar=slope, in1=e, op0=ALU.mult, op1=ALU.max))
                nc.vector.scalar_tensor_tensor(out=e3, in0=e3, scalar=neg, in1=QB[:, 2 * D:4 * D].unsqueeze(1).broadcast_to([D, 4, 2 * D]),
                                               op0=ALU.add, op1=ALU.subtract).then_inc(f_ie, 1)

            def score(l, p):
                heads, slope, _ = LAYERS[l]
                n, S = l * PAIRS + p, ROOM[p]
                dve.wait_ge(f_g[n % NB], reach[n])
                g, w = buf(n, p), wts(n, p, heads)
                m = mx[n % NB][:, 0:2 * heads].rearrange("p (t h) -> p t h", t=2)
                for t in range(2):
                    q = QS[:, 2 * p + t, 0:heads] if l < 3 else SX[:, 2 * p + t, D:D + 1]
                    last = nc.vector.tensor_tensor(w[:, t, :, :], g[:, t, :, D:D + heads],
                                                   q.unsqueeze(1).broadcast_to([D, S, heads]), ALU.add)
                ch.link(last)
                flat = WT4[n % NB][:, 0:2 * S * heads]
                ch.link(nc.vector.scalar_tensor_tensor(out=flat, in0=flat, scalar=slope, in1=flat, op0=ALU.mult, op1=ALU.max))
                if S > 1:
                    for t in range(2):
                        last = nc.vector.tensor_tensor(w[:, t, :, :], w[:, t, :, :],
                                                       PEN[:, 2 * p + t, 0:S].unsqueeze(2).broadcast_to([D, S, heads]), ALU.add)
                    ch.link(last)
                ch.link(nc.vector.tensor_reduce(m, w.rearrange("p t s h -> p t h s"), AX.X, ALU.max))
                for t in range(2):
                    last = nc.vector.tensor_tensor(w[:, t, :, :], w[:, t, :, :],
                                                   m[:, t, :].unsqueeze(1).broadcast_to([D, S, heads]), ALU.subtract)
                last.then_inc(f_e, 1)

            def weigh(l, p):
                heads = LAYERS[l][0]
                n, S = l * PAIRS + p, ROOM[p]
                dve.wait_ge(f_w, n + 1)
                g, w = buf(n, p), wts(n, p, heads)
                m = mx[n % NB][:, 0:2 * heads].rearrange("p (t h) -> p t h", t=2)
                ch.link(nc.vector.tensor_reduce(m, w.rearrange("p t s h -> p t h s"), AX.X, ALU.add))
                ch.link(nc.vector.reciprocal(m, m))
                for t in range(2):
                    last = nc.vector.tensor_tensor(w[:, t, :, :], w[:, t, :, :],
                                                   m[:, t, :].unsqueeze(1).broadcast_to([D, S, heads]), ALU.mult)
                ch.link(last)
                if l == 0:
                    nc.vector.tensor_copy(IDX[:, 2 * p:2 * p + 2, 0:S], g[:, :, :, D + 1])
                for t in range(2):
                    v = g[:, t, :, 0:D].rearrange("p s (h d) -> p s h d", h=heads)
                    last = nc.vector.tensor_tensor(v, v, w[:, t, :, :].unsqueeze(3).broadcast_to([D, S, heads, D // heads]), ALU.mult)
                ch.link(last)
                dst = SX[:, 2 * p:2 * p + 2, D:2 * D] if l == 2 else AGP[n % NB]
                ins = nc.vector.tensor_reduce(dst, g[:, :, :, 0:D].rearrange("p t s d -> p t d s"), AX.X, ALU.add)
                ins.then_inc(f_gfree, 1)
                dve.wait_ge(f_gfree, n + 1)
                if l == 0 and p == PAIRS - 1:
                    dve.wait_ge(f_im, 16)
                    for t in range(2):
                        ch.link(nc.vector.reciprocal(small[:, 8:9], psD[t][:, D:D + 1]))
                        ch.link(nc.vector.tensor_scalar(UE[0][:, t, :], psD[t][:, 0:D], small[:, 8:9], None, ALU.mult))
                        ch.link(nc.vector.tensor_tensor(UE[0][:, t, :], UE[0][:, t, :], dst[:, t, :], ALU.subtract))
                        ch.link(nc.vector.scalar_tensor_tensor(out=dst[:, t, :], in0=UE[0][:, t, :], scalar=ISO[:, t:t + 1],
                                                               in1=dst[:, t, :], op0=ALU.mult, op1=ALU.add))
                if l == 1:
                    nc.vector.tensor_scalar(UE[p % 2], dst, 0.0, None, ALU.min).then_inc(f_t, 1)
                if l == 2:
                    nc.vector.tensor_copy(small[:, 9:10], SX[:, 2 * p + 1, 2 * D - 1:2 * D]).then_inc(f_agg2, 1)

            def residual(l, p, m):
                n = l * PAIRS + p
                if l == 2:
                    xp = XN[:, 2 * p:2 * p + 2, :]
                    h, b = 2 * p // 16, 2 * p % 16
                    for t in range(2):
                        last = nc.vector.tensor_tensor(xp[:, t, :].rearrange("p (k d) -> p k d", k=4),
                                                       xp[:, t, :].rearrange("p (k d) -> p k d", k=4),
                                                       AGL[:, b + t, :, 32 * h:32 * h + 32], ALU.add)
                    ch.link(last)
                else:
                    xp = SX[:, 2 * p:2 * p + 2, 0:D]
                    ag = AGP[n % NB]
                    if l == 0:
                        ch.link(nc.vector.tensor_tensor(xp, xp, ag, ALU.add))
                    else:
                        ch.link(nc.vector.scalar_tensor_tensor(out=xp, in0=ag, scalar=0.0, in1=xp, op0=ALU.max, op1=ALU.add))
                    if l == 1:
                        dve.wait_ge(f_u, p + 1)
                        ch.link(nc.vector.scalar_tensor_tensor(out=xp, in0=UE[p % 2], scalar=-1.0, in1=xp, op0=ALU.add, op1=ALU.add))
                for t in range(2):
                    last = nc.vector.bn_stats(st6[:, t, :], xp[:, t, :])
                ch.link(last)
                for t in range(2):
                    last = nc.vector.bn_aggr(mv[m % NB][:, t, :], st6[:, t, :])
                ch.link(last)
                nc.vector.tensor_scalar(ve[m % NB], mv[m % NB][:, :, 1], EPS, None, ALU.add).then_inc(f_var, 1)

            def norm(l, p, m):
                dve.wait_ge(f_rs, m + 1)
                xp = XN[:, 2 * p:2 * p + 2, :] if l == 2 else SX[:, 2 * p:2 * p + 2, 0:D]
                for t in range(2):
                    last = nc.vector.tensor_scalar(xp[:, t, :], xp[:, t, :], mv[m % NB][:, t, 0:1], ve[m % NB][:, t:t + 1],
                                                   ALU.subtract, ALU.mult)
                last.then_inc(f_x, 1)

            for l in range(4):
                if l == 3:
                    dve.wait_ge(f_self, 16 * T)
                for q in range(PAIRS + 3):
                    if l == 0 and 4 <= q < 20:
                        iso(q - 4)
                    if q < PAIRS:
                        score(l, q)
                    if 1 <= q <= PAIRS:
                        weigh(l, q - 1)
                    if l != 2:
                        if 2 <= q <= PAIRS + 1:
                            residual(l, q - 2, l * PAIRS + q - 2)
                        if q >= 3:
                            norm(l, q - 3, l * PAIRS + q - 3)
                if l == 2:
                    dve.wait_ge(f_natl, 16 * 5)
                    for q in range(PAIRS + 1):
                        if q < PAIRS:
                            residual(2, q, 2 * PAIRS + q)
                        if q >= 1:
                            norm(2, q - 1, 2 * PAIRS + q - 1)

        with nc.Block() as block:
            @block.gpsimd
            def _(pool):
                full = pool.value_load(bad_i[0:1, 0:1], min_val=0, max_val=1)
                with pool.If(full == 0):
                    fast_gpsimd(pool)

            @block.sync
            def _(sp):
                full = sp.value_load(bad_i[0:1, 0:1], min_val=0, max_val=1)
                with sp.If(full == 0):
                    fast_sync(sp)
                with sp.Else():
                    dense_sync(sp)

            @block.tensor
            def _(pe):
                full = pe.value_load(bad_i[0:1, 0:1], min_val=0, max_val=1)
                with pe.If(full == 0):
                    fast_tensor(pe)
                with pe.Else():
                    dense_tensor(pe)

            @block.scalar
            def _(act):
                full = act.value_load(bad_i[0:1, 0:1], min_val=0, max_val=1)
                with act.If(full == 0):
                    fast_scalar(act)
                with act.Else():
                    dense_scalar(act)

            @block.vector
            def _(dve):
                full = dve.value_load(bad_i[0:1, 0:1], min_val=0, max_val=1)
                with dve.If(full == 0):
                    fast_vector(dve)
                with dve.Else():
                    dense_vector(dve)


_INS = ['x', 'adj', 'L0_gnn_attn', 'L1_gnn_W', 'L1_gnn_a', 'L2_gnn_W', 'L2_gnn_a', 'L3_gnn_W', 'L3_gnn_a']
_OUTS = [((8192, 128), 'float32')]


def kernel(**inputs):
    import numpy as _np
    import concourse.bacc as _bacc
    from concourse import mybir as _mybir
    from concourse.bass_utils import run_bass_kernel_spmd as _run

    nc = _bacc.Bacc("TRN2", target_bir_lowering=False, num_devices=1)
    arrays, args = {}, []
    for name in _INS:
        a = _np.ascontiguousarray(inputs[name])
        arrays[f"in_{name}_dram"] = a
        args.append(nc.dram_tensor(f"in_{name}_dram", a.shape, _mybir.dt.from_np(a.dtype), kind="ExternalInput").ap())
    for i, (shape, dtype) in enumerate(_OUTS):
        dt = _mybir.dt.from_np(_np.dtype(dtype))
        args.append(nc.dram_tensor(f"out_{i}_dram", shape, dt, kind="ExternalOutput").ap())
    build_program(nc, *args)
    r = _run(nc, [arrays], core_ids=[0])
    got = tuple(r.results[0][f"out_{i}_dram"] for i in range(len(_OUTS)))
    return got[0]
```

```python
import concourse.bass as bass
from concourse import mybir
from contextlib import ExitStack

f32 = mybir.dt.float32
bf16 = mybir.dt.bfloat16
i32 = mybir.dt.int32
ALU = mybir.AluOpType
ACT = mybir.ActivationFunctionType
AX = mybir.AxisListType

N = 8192
D = 128
T = N // D
KEY, QRY = D, D + 4
WX = D + 8
EPS = 1e-5
LAYERS = [(1, 0.2, -1e9), (1, 0.2, -1e9), (4, 0.2, -9e15), (1, 0.01, -9e16)]
SLOTS = 16
PACK = 8
WORDS = N // PACK
SEGS = 8
SEG = WORDS // SEGS
HALF = N // 2
SHIFT = (2 ** PACK - 1) * (WORDS // 2)
PROFILE = [(1, 16), (1, 10), (2, 8), (4, 7), (8, 6), (10, 5), (12, 4), (12, 3), (10, 2), (4, 1)]
ROOM = [s for n, s in PROFILE for _ in range(n)]
PAIRS = T // 2
assert len(ROOM) == T
BIG = 1e30
TW = D + 4
RW = D + SLOTS + 4
R_SLOT, R_Q0, R_Q1, R_ID = D, D + SLOTS, D + SLOTS + 1, D + SLOTS + 2
TW0 = D + 2
RX = RW + TW0
FEW = 8
assert max(ROOM[2:]) <= FEW
FORCE = None
GRP = 4


class Chain:

    def __init__(self, eng, sem):
        self.eng, self.sem, self.base, self.count = eng, sem, 0, 0

    def loop(self, i, per):
        self.start, self.per = self.count, per
        self.base = i * per

    def endloop(self, trips):
        assert self.count - self.start == self.per, (self.count - self.start, self.per)
        self.base, self.count = 0, self.start + self.per * trips

    def add(self, ins):
        self.count += 1
        ins.then_inc(self.sem, 1)

    def wait(self):
        self.eng.wait_ge(self.sem, self.base + self.count)

    def link(self, ins):
        self.add(ins)
        self.wait()


def build_program(nc, x, adj, L0_attn, L1_W, L1_a, L2_W, L2_a, L3_W, L3_a, out):
    ctx = ExitStack()
    with ctx:
        def sb(name, shape, dt=f32):
            return ctx.enter_context(nc.sbuf_tensor(name, shape, dt))

        def pb(name, shape, dt=f32):
            return ctx.enter_context(nc.psum_tensor(name, shape, dt))

        def sem(name):
            return ctx.enter_context(nc.semaphore(name))

        ident = sb("ident", [D, D])
        ones = sb("ones", [D, D])
        Wext = sb("Wext", [D, 4, WX])
        W2nat = sb("W2nat", [D, D])
        WT = sb("WT", [D, 2, D])
        A1 = sb("A1", [D, 2])
        A2 = sb("A2", [D, 8])
        A3 = sb("A3", [D, 2])
        small = sb("small", [D, 16])
        strict = sb("strict", [D, D])
        bad = sb("bad", [D, 2])
        bad_i = sb("bad_i", [D, 1], i32)
        rank1 = sb("rank1", [D, T])
        rank_i = sb("rank_i", [D, T], i32)
        keys0 = sb("keys0", [D, T])
        qrys0 = sb("qrys0", [D, T])
        arena = sb("arena", [D, 50688])

        class Place:

            def __init__(self, at=0):
                self.at = at

            def take(self, *shape, dt=f32):
                n = 1
                for k in shape:
                    n *= k
                words = n if dt in (f32, i32) else n // 2
                v = arena[:, self.at:self.at + words]
                self.at += words
                assert self.at <= 50688, self.at
                if dt != f32:
                    v = v.bitcast(dt)
                if len(shape) == 2:
                    v = v.rearrange("p (a b) -> p a b", b=shape[1])
                if len(shape) == 3:
                    v = v.rearrange("p (a b c) -> p a b c", b=shape[1], c=shape[2])
                return v

        place = Place()
        X = place.take(T, D)
        AG = place.take(T, D)
        WH = place.take(T, WX)
        KB = place.take(N)
        E = place.take(N)
        A = place.take(N, dt=i32)
        PT = place.take(2, GRP * D)
        xT = PT[:, 0, 0:D]
        diag = PT[:, 1, 0:D]
        xs = PT[:, 0, D:2 * D]

        NS = 4
        TOP = 50688 - 2 * 2 * D - NS * 2 * TW - TW
        place = Place(TOP)
        sT = [place.take(2 * D) for _ in range(2)]
        stage = [place.take(2, TW) for _ in range(NS)]
        row0 = place.take(TW)

        place = Place()
        R = place.take(T, RX)
        REC = R[:, :, 0:RW]
        X0 = R[:, :, RW:RX]
        scan_end = place.at
        ADJ = [place.take(HALF, dt=i32) for _ in range(4)]
        SIGN = [place.take(HALF, dt=bf16) for _ in range(2)]
        power = place.take(PACK, D, dt=bf16)
        ones_b = place.take(D, dt=bf16)
        count_b = place.take(WORDS, dt=bf16)
        mask = place.take(PACK, dt=i32)
        first = place.take(PACK)
        degs = place.take(8)
        less_half = place.take(1)
        top8 = place.take(2, 8 * SEGS)
        rest8 = place.take(2, 8 * SEGS)
        word16 = place.take(2, SLOTS)
        key16 = place.take(2 * SLOTS, dt=i32)
        col16 = place.take(2 * SLOTS, dt=i32)
        bits = place.take(2 * SLOTS, PACK, dt=i32)
        cand = place.take(2 * SLOTS, PACK)
        rest = place.take(2, SLOTS * PACK)
        top16 = place.take(2, SLOTS)
        found = place.take(2, SLOTS)
        deg2 = place.take(2)
        nfound = place.take(2)
        wrong = place.take(2)
        deg = place.take(T)
        NC = SLOTS + 1
        cls = place.take(NC, T)
        cnt = place.take(NC)
        off = place.take(NC)
        tot = place.take(NC)
        roomy = place.take(NC)
        G0 = [place.take(2, FEW, TW) for _ in range(2)]
        ix0 = [place.take(2, FEW, dt=i32) for _ in range(2)]
        pen0 = [place.take(2, FEW) for _ in range(2)]
        w0 = [place.take(2, FEW) for _ in range(2)]
        m0 = place.take(2)
        ag0 = place.take(2, D)
        st0 = place.take(2, 6)
        mv0 = [place.take(2, 2) for _ in range(2)]
        ve0 = [place.take(2) for _ in range(2)]
        ln0 = [place.take(2) for _ in range(2)]
        x1 = [place.take(2, D) for _ in range(2)]
        a_row = place.take(2, D)
        assert place.at <= TOP, place.at
        product = G0[1].rearrange("p t s w -> p (t s w)")[:, 0:T // 4 * D].rearrange("p (t d) -> p t d", d=D)
        count_f = G0[0].rearrange("p t s w -> p (t s w)")[:, 0:WORDS]
        sort_place = Place(scan_end)
        ind = sort_place.take(NC, T)
        run = sort_place.take(NC, T)

        place = Place(scan_end)
        SX = R
        IDX = place.take(T, SLOTS, dt=i32)
        IDN = place.take(T, SLOTS, dt=i32)
        PEN = place.take(T, SLOTS)
        QS = place.take(T, 4)
        RID = place.take(T, dt=i32)
        RID1 = place.take(4, dt=i32)
        ISO = place.take(2)
        GW = 2 * SLOTS * TW
        G_AT = place.at
        NB = 4
        G = [place.take(GW) for _ in range(3)]
        G.append(place.take(GW // 2))
        AGP = [place.take(2, D) for _ in range(NB)]
        WT4 = [place.take(2 * SLOTS * 4) for _ in range(NB)]
        mx = [place.take(2 * 4) for _ in range(NB)]
        UE = [place.take(2, D) for _ in range(2)]
        st6 = [place.take(2, 6) for _ in range(2)]
        mv = [place.take(2, 2) for _ in range(NB)]
        ve = [place.take(2) for _ in range(NB)]
        lnv = [place.take(2) for _ in range(NB)]
        csum = place.take(1)
        eps_col = place.take(1)
        x_sums = place.take(PAIRS)
        sum_row = place.take(D)
        EE = place.take(4, 4 * 2 * D)
        q_col = place.take(2)
        q_part = place.take(3, T, dt=bf16)
        q_rest = place.take(T)
        MARK = place.take(8, 2 * D, dt=bf16)
        QB = place.take(4 * D)
        place_n = place.take(2 * D)
        ends = place.take(2, 2, 3)
        assert place.at <= TOP, place.at
        XN = R[:, :, RW:RW + D + 1]
        AGL = arena[:, G_AT:G_AT + T * D].rearrange("p (b k f) -> p b k f", k=4, f=D)

        banks = pb("banks", [D, 8 * 512])
        psA, psB, psT0, psT1, acc, psD0, psD1, psS = (banks[:, 512 * k:512 * (k + 1)] for k in range(8))
        psT, psD = [psT0, psT1], [psD0, psD1]
        PK = [banks[:, 4 * 512:4 * 512 + WORDS], banks[:, 6 * 512:6 * 512 + WORDS]]

        s_load = sem("setup_loads")
        s_id = sem("identity_ready")
        s_zero = sem("weights_zeroed")
        s_wt = sem("weights_transposed")
        s_wtc = sem("transposes_copied")
        s_wa = sem("score_weights_ready")
        s_setup = sem("setup_done")

        s_const = sem("constants_ready")
        s_x = [sem(f"x_loaded{c}") for c in range(4)]
        s_xz = sem("x_transposed")
        s_xzc = sem("xT_copied")
        s_pj = sem("x_projected")
        s_pjc = sem("projection_copied")
        s_tab0 = sem("table0_written")
        s_arow = sem("attention_rows_loaded")
        s_dot = sem("last_quarter_multiplied")
        s_red = sem("last_quarter_summed")
        s_adj = [sem(f"adjacency_loaded{i}") for i in range(4)]
        s_sign = sem("signs_ready")
        s_pconst = sem("powers_ready")
        s_packed = sem("half_packed")
        s_picked = sem("tile_picked")
        s_dec = sem("pair_of_tiles_decoded")
        s_fch = sem("search_chain")
        s_cnt = sem("classes_counted")
        s_cntm = sem("counts_added")
        s_rank = sem("ranks_ready")
        s_bad = sem("row_flags_ready")
        s_badm = sem("flags_added")

        l_idx = sem("l0_slots_ready")
        l_g = [sem(f"l0_gathered{i}") for i in range(2)]
        l_free = sem("l0_gather_buffer_free")
        l_e = sem("l0_scores_ready")
        l_w = sem("l0_weights_ready")
        l_var = sem("l0_variance_ready")
        l_ln = sem("l0_log_ready")
        l_rs = sem("l0_rstd_ready")
        l_x = sem("l0_normed")
        l_xT = sem("l0_transposed")
        l_xTc = sem("l0_T_copied")
        l_pr = sem("l1_projected")
        l_pc = sem("l1_projection_copied")
        l_tab = [sem(f"table1_written{i}") for i in range(2)]
        s_row0 = sem("table0_row0_written")
        s_zrow = sem("row0_zeroed")
        f_fconst = sem("sparse_constants_ready")
        f_oh = sem("last_queries_marked")
        f_ohm = sem("last_queries_spread")
        f_qb = sem("last_queries_steps")
        f_ia = sem("isolated_sums_ready")
        f_il = sem("isolated_slopes_ready")
        f_fix = [sem(f"table1_rows_corrected{i}") for i in range(2)]
        f_cs = sem("features_summed")
        f_csc = sem("feature_sums_copied")
        f_rest = sem("other_records_loaded")
        f_scat = sem("records_sorted")
        f_rec = sem("records_loaded")
        f_rank = sem("rank_column_written")
        f_idx = sem("slots_ready")
        f_g = [sem(f"neighbours_gathered{i}") for i in range(NB)]
        f_gfree = sem("gather_buffer_free")
        f_e = sem("scores_ready")
        f_w = sem("weights_ready")
        f_t = sem("elu_min_ready")
        f_u = sem("elu_exp_ready")
        f_var = sem("variance_ready")
        f_ln = sem("log_ready")
        f_rs = sem("rstd_ready")
        f_x = sem("pair_normed")
        f_xT = sem("pair_transposed")
        f_xTc = sem("pair_T_copied")
        f_pr = sem("pair_projected")
        f_pc = sem("pair_projection_copied")
        f_mn = sem("mean_added")
        f_row0 = sem("mean_row_ready")
        f_tab = [sem(f"table_written{i}") for i in range(NS)]
        f_tab0 = sem("mean_row_written")
        f_ch = sem("sparse_dve_chain")
        f_km = sem("kmax_steps_pe")
        f_kd = sem("kmax_steps_dve")
        f_ie = sem("isolated_scores_ready")
        f_ip = sem("isolated_probs_ready")
        f_im = sem("isolated_multiplied")
        f_agg2 = sem("layer2_sums_ready")
        f_nat = sem("layer2_scattered")
        f_natl = [sem(f"layer2_loaded{i}") for i in range(4)]
        f_added = sem("layer2_sums_added")
        f_xq = sem("layer3_rows_written")
        f_out = sem("output_rows_written")

        d_x = sem("dense_x_loaded")
        d_xs = sem("dense_x_staged")
        d_xT = sem("dense_x_transposed")
        d_xTc = sem("dense_xT_copied")
        d_pr = sem("dense_projected")
        d_wh = sem("dense_projection_copied")
        d_diag = sem("dense_diag_ready")
        d_kb = sem("dense_keys_spread")
        d_kbc = sem("dense_keys_copied")
        d_adj = sem("dense_adj_loaded")
        d_e = sem("dense_scores_ready")
        d_p = sem("dense_probs_ready")
        d_tr = sem("dense_probs_transposed")
        d_pt = sem("dense_PT_copied")
        d_mm = sem("dense_group_multiplied")
        d_out = sem("dense_tile_normed")
        d_el = sem("dense_elu_exp")
        d_bh = sem("dense_rows_regrouped")
        d_ex = sem("dense_elu_exp_ready")
        d_var = sem("dense_variance_ready")
        d_ln = sem("dense_log_ready")
        d_rs = sem("dense_rstd_ready")
        d_lay = sem("dense_layer_done")
        d_ch = sem("dense_dve_chain")
        d_store = sem("dense_out_stored")

        tables = [nc.dram_tensor(f"table{l}", (N + 1, TW if l else TW0), f32).ap() for l in range(4)]
        sorted_rec = nc.dram_tensor("records_in_order", (N + 1, RW), f32).ap()
        layer2_nat = nc.dram_tensor("layer2_by_node", (N, 2 * D), f32).ap()
        rows3 = nc.dram_tensor("layer3_rows", (N, D + 1), f32).ap()

        adj_units = adj.rearrange("(i t p) (h c) -> i t h p c", t=2, p=D, h=2)

        def unit(i, u):
            if type(i) is int:
                return adj_units[i, u // 2, u % 2, :, :]
            return adj_units[bass.ds(i, 1), u // 2, u % 2, :, :].rearrange("o p c -> p (o c)")

        def quarter(c):
            return slice(c * T // 4, (c + 1) * T // 4)

        def table1_rows(p):
            if type(p) is int:
                return tables[1][1 + 2 * p * D:1 + 2 * (p + 1) * D, :].rearrange("(t p) w -> p t w", p=D)
            rows = tables[1][1:N + 1, :].rearrange("(m t p) w -> m p t w", t=2, p=D)
            return rows[bass.ds(p, 1), :, :, :].rearrange("o p t w -> p (o t) w")

        with nc.Block() as block:
            @block.gpsimd
            def _(pool):
                nc.gpsimd.memset(ident[:], 1.0).then_inc(s_zero, 1)
                nc.gpsimd.memset(ones[:], 1.0).then_inc(s_zero, 1)
                nc.gpsimd.memset(A2[:], 0.0).then_inc(s_zero, 1)
                nc.gpsimd.memset(Wext[:], 0.0).then_inc(s_zero, 1)
                pool.wait_ge(s_zero, 4)
                nc.gpsimd.affine_select(out=ident[:], in_=ident[:], compare_op=ALU.is_equal, fill=0.0, base=0,
                                        pattern=[[-1, D]], channel_multiplier=1).then_inc(s_id, 1)

            @block.sync
            def _(sp):
                sp.wait_ge(s_zero, 4)
                sp.dma_start(Wext[:, 0, KEY:KEY + 1], L0_attn[D:2 * D, :]).then_inc(s_load, 16)
                sp.dma_start(Wext[:, 0, QRY:QRY + 1], L0_attn[0:D, :]).then_inc(s_load, 16)
                sp.dma_start(Wext[:, 1, 0:D], L1_W).then_inc(s_load, 16)
                for k in range(2):
                    rows = slice(k * D, (k + 1) * D)
                    sp.dma_start(A1[:, k:k + 1], L1_a[rows].rearrange("(p o) -> p o", o=1)).then_inc(s_load, 16)
                    sp.dma_start(A3[:, k:k + 1], L3_a[rows, :]).then_inc(s_load, 16)
                sp.dma_start(Wext[:, 2, 0:D].rearrange("i (h d) -> i h d", h=4),
                             L2_W.rearrange("h i d -> i h d")).then_inc(s_load, 16)
                for h in range(4):
                    rows = slice(32 * h, 32 * h + 32)
                    sp.dma_start(A2[rows, h:h + 1], L2_a[h, 0:32, :]).then_inc(s_load, 16)
                    sp.dma_start(A2[rows, 4 + h:5 + h], L2_a[h, 32:64, :]).then_inc(s_load, 16)
                sp.dma_start(W2nat[:], L3_W).then_inc(s_load, 16)
                sp.dma_start(a_row, L0_attn.rearrange("(k d) o -> o k d", k=2).broadcast_to([D, 2, D])).then_inc(s_arow, 16)
                sp.wait_ge(s_x[3], 16)
                for u in range(4):
                    sp.dma_start(ADJ[u], unit(0, u)).then_inc(s_adj[u], 16)

            @block.scalar
            def _(act):
                for c in range(4):
                    act.dma_start(X0[:, quarter(c), 0:D], x.rearrange("(t p) d -> p t d", p=D)[:, quarter(c), :]).then_inc(s_x[c], 16)

            @block.tensor
            def _(pe):
                pe.wait_ge(s_id, 1)
                pe.wait_ge(s_load, 17 * 16)
                nc.tensor.transpose(psA[:, 0:D], Wext[:, 1, 0:D], ident[:])
                nc.tensor.transpose(psA[:, D:2 * D], Wext[:, 2, 0:D], ident[:])
                nc.tensor.transpose(psA[:, 2 * D:3 * D], W2nat[:], ident[:]).then_inc(s_wt, 1)
                pe.wait_ge(s_wtc, 1)
                nc.tensor.matmul(psB[:, 0:2], WT[:, 0, :], A1[:], start=True, stop=True)
                nc.tensor.matmul(psB[:, 8:16], WT[:, 1, :], A2[:], start=True, stop=True)
                nc.tensor.matmul(psB[:, 16:18], W2nat[:], A3[:], start=True, stop=True).then_inc(s_wa, 1)

            @block.vector
            def _(dve):
                dve.wait_ge(s_wt, 1)
                nc.vector.tensor_copy(WT[:, :, :], psA[:, 0:2 * D].rearrange("p (k d) -> p k d", k=2)).then_inc(s_wtc, 1)
                nc.vector.tensor_copy(Wext[:, 3, 0:D], psA[:, 2 * D:3 * D])
                nc.vector.tensor_copy(Wext[:, 0, 0:D], ident[:])
                dve.wait_ge(s_wa, 1)
                nc.vector.tensor_copy(Wext[:, 1, KEY:KEY + 1], psB[:, 0:1])
                nc.vector.tensor_copy(Wext[:, 1, QRY:QRY + 1], psB[:, 1:2])
                nc.vector.tensor_copy(Wext[:, 2, KEY:KEY + 8], psB[:, 8:16])
                nc.vector.tensor_copy(Wext[:, 3, QRY:QRY + 1], psB[:, 16:17])
                nc.vector.tensor_copy(Wext[:, 3, KEY:KEY + 1], psB[:, 17:18]).then_inc(s_setup, 1)
                dve.wait_ge(s_setup, 1)

        passes = [(l, h) for l, (heads, _, _) in enumerate(LAYERS) for h in range(heads)]
        GROUPS = T // GRP
        HEADS_END = sum(heads for heads, _, _ in LAYERS[:3]) - 1
        by_head = nc.dram_tensor("sums_by_head", (4, N, D // 4), f32).ap()
        LAY_LINKS = [0, 6, 0, 1]

        def dense_sync(sp):
            sp.wait_ge(f_scat, 16 * 2 * EARLY)
            sp.dma_start(X[:], x.rearrange("(t p) d -> p t d", p=D)).then_inc(d_x, 16)
            for n in range(len(passes)):
                if n:
                    sp.wait_ge(d_e, n * T)
                sp.dma_start(A[:], adj[0:D, :]).then_inc(d_adj, 16)
                with sp.Fori(1, T) as t:
                    sp.wait_ge(d_e, t + n * T)
                    sp.dma_start(A[:], adj.rearrange("(t p) j -> t p j", p=D)[bass.ds(t, 1), :, :].rearrange("o p j -> p (o j)")).then_inc(d_adj, 16)
                if n == HEADS_END:
                    sp.wait_ge(d_out, (n + 1) * T)
                    heads = LAYERS[2][0]
                    for h in range(heads):
                        sp.dma_start(by_head.rearrange("h (t p) d -> h p t d", p=D)[h],
                                     AG[:, :, h * (D // heads):(h + 1) * (D // heads)]).then_inc(d_bh, 16)
                    sp.wait_ge(d_bh, 16 * heads)
                    sp.dma_start(AG[:], by_head.rearrange("h (m k) d -> (h m) (k d)", k=heads)
                                 .rearrange("(t p) f -> p t f", p=D)).then_inc(d_bh, 16)
            sp.wait_ge(d_lay, len(LAYERS))
            sp.dma_start(out.rearrange("(t p) d -> p t d", p=D), X[:]).then_inc(d_store, 16)
            sp.wait_ge(d_store, 16)

        def dense_tensor(pe):
            n = 0
            for l, (heads, _, _) in enumerate(LAYERS):
                with pe.Fori(0, T) as t:
                    pe.wait_ge(d_xs, t + (l * T + 1))
                    nc.tensor.transpose(psA[:, 0:D], xs, ident[:]).then_inc(d_xT, 1)
                    pe.wait_ge(d_xTc, t + (l * T + 1))
                    nc.tensor.matmul(psB[:, 0:WX], xT, Wext[:, l, :], start=True, stop=True).then_inc(d_pr, 1)
                    pe.wait_ge(d_wh, t + (l * T + 1))
                for h in range(heads):
                    dh = D // heads
                    with pe.Fori(0, T) as t:
                        pe.wait_ge(d_diag, t + (n * T + 1))
                        nc.tensor.matmul(psA[:, 0:D], ones[:], diag, start=True, stop=True).then_inc(d_kb, 1)
                        pe.wait_ge(d_kbc, t + (n * T + 1))
                    with pe.Fori(0, T) as t:
                        pe.wait_ge(d_p, t + (n * T + 1))
                        if n:
                            pe.wait_ge(d_out, t + n * T)
                        else:
                            pe.wait_ge(d_kbc, T)
                        for g in range(GROUPS):
                            for j in range(g * GRP, (g + 1) * GRP):
                                last = nc.tensor.transpose(psT[g % 2][:, j % GRP * D:(j % GRP + 1) * D],
                                                           E[:, j * D:(j + 1) * D], ident[:])
                            last.then_inc(d_tr, 1)
                            pe.wait_ge(d_pt, t * GROUPS + (n * T * GROUPS + g + 1))
                            for j in range(g * GRP, (g + 1) * GRP):
                                last = nc.tensor.matmul(acc[:, 0:dh], PT[:, g % 2, j % GRP * D:(j % GRP + 1) * D],
                                                        WH[:, j, h * dh:(h + 1) * dh],
                                                        start=(j == 0), stop=(j == T - 1))
                            last.then_inc(d_mm, 1)
                    n += 1

        def dense_scalar(act):
            n = 0
            for l, (heads, _, _) in enumerate(LAYERS):
                if l:
                    act.wait_ge(d_lay, l)
                else:
                    act.wait_ge(d_x, 16)
                with act.Fori(0, T) as t:
                    nc.scalar.copy(xs, X[:, bass.ds(t, 1), :].rearrange("p o d -> p (o d)")).then_inc(d_xs, 1)
                    act.wait_ge(d_xT, t + (l * T + 1))
                    nc.scalar.copy(xT, psA[:, 0:D]).then_inc(d_xTc, 1)
                    act.wait_ge(d_pr, t + (l * T + 1))
                    nc.scalar.copy(WH[:, bass.ds(t, 1), :].rearrange("p o d -> p (o d)"), psB[:, 0:WX]).then_inc(d_wh, 1)
                for h in range(heads):
                    with act.Fori(0, T) as t:
                        act.wait_ge(d_kb, t + (n * T + 1))
                        nc.scalar.copy(KB[:, bass.ds(t * D, D)], psA[:, 0:D]).then_inc(d_kbc, 1)
                    with act.Fori(0, T) as t:
                        act.wait_ge(d_e, t + (n * T + 1))
                        nc.scalar.activation(E[:], E[:], ACT.Exp, bias=small[:, 1:2], accum_out=small[:, 2:3]).then_inc(d_p, 1)
                        with act.Fori(0, GROUPS // 2) as g:
                            for b in range(2):
                                at = t * GROUPS + g * 2 + (n * T * GROUPS + b)
                                act.wait_ge(d_tr, at + 1)
                                nc.scalar.copy(PT[:, b, :], psT[b]).then_inc(d_pt, 1)
                    n += 1
                with act.Fori(0, T) as t:
                    if l == 1:
                        act.wait_ge(d_el, t + 1)
                        nc.scalar.activation(E[:, 0:D], E[:, 0:D], ACT.Exp).then_inc(d_ex, 1)
                    act.wait_ge(d_var, t + (l * T + 1))
                    nc.scalar.activation(small[:, 9:10], small[:, 8:9], ACT.Ln).then_inc(d_ln, 1)
                    act.wait_ge(d_ln, t + (l * T + 1))
                    nc.scalar.activation(small[:, 8:9], small[:, 9:10], ACT.Exp, scale=-0.5).then_inc(d_rs, 1)

        def dense_vector(dve):
            ch = Chain(dve, d_ch)
            n = 0
            for l, (heads, slope, neg) in enumerate(LAYERS):
                dve.wait_ge(d_wh, (l + 1) * T)
                for h in range(heads):
                    dh = D // heads
                    with dve.Fori(0, T) as t:
                        if n:
                            dve.wait_ge(d_kbc, t + n * T)
                            dve.wait_ge(d_mm, n * T * GROUPS)
                        else:
                            dve.wait_ge(d_xTc, T)
                        nc.vector.tensor_scalar(diag, ident[:], WH[:, bass.ds(t, 1), KEY + h:KEY + h + 1].rearrange("p o d -> p (o d)"),
                                                None, ALU.mult).then_inc(d_diag, 1)
                        dve.wait_ge(d_kb, t + (n * T + 1))
                    dve.wait_ge(d_kbc, (n + 1) * T)
                    with dve.Fori(0, T) as t:
                        ch.loop(t, 9 if l else 8)
                        ch.link(nc.vector.tensor_scalar(E[:], KB[:], WH[:, bass.ds(t, 1), QRY + h:QRY + h + 1].rearrange("p o d -> p (o d)"),
                                                        None, ALU.add))
                        ch.link(nc.vector.scalar_tensor_tensor(out=E[:], in0=E[:], scalar=slope, in1=E[:], op0=ALU.mult, op1=ALU.max))
                        dve.wait_ge(d_adj, t * 16 + (n * T + 1) * 16)
                        M = A[:].bitcast(f32)
                        ch.link(nc.vector.tensor_scalar(M, A[:], 0.0, None, ALU.is_gt))
                        if l:
                            ch.link(nc.vector.tensor_tensor(E[:], E[:], M, ALU.mult))
                        ch.link(nc.vector.tensor_scalar(M, M, 1.0, -neg, ALU.subtract, ALU.mult))
                        ch.link(nc.vector.tensor_tensor(E[:], E[:], M, ALU.add))
                        ch.link(nc.vector.reduce_max(small[:, 0:1], E[:], AX.X))
                        nc.vector.tensor_scalar(small[:, 1:2], small[:, 0:1], -1.0, None, ALU.mult).then_inc(d_e, 1)
                        dve.wait_ge(d_mm, t * GROUPS + (n * T + 1) * GROUPS)
                        ch.link(nc.vector.reciprocal(small[:, 3:4], small[:, 2:3]))
                        ch.link(nc.vector.tensor_scalar(AG[:, bass.ds(t, 1), h * dh:(h + 1) * dh].rearrange("p o d -> p (o d)"),
                                                        acc[:, 0:dh], small[:, 3:4], None, ALU.mult))
                        nc.vector.tensor_copy(small[:, 4:5], small[:, 3:4]).then_inc(d_out, 1)
                        ch.endloop(T)
                    n += 1
                if l == 2:
                    dve.wait_ge(d_bh, 16 * (heads + 1))
                with dve.Fori(0, T) as t:
                    ag = AG[:, bass.ds(t, 1), :].rearrange("p o d -> p (o d)")
                    xt = X[:, bass.ds(t, 1), :].rearrange("p o d -> p (o d)")
                    ch.loop(t, {0: 0, 1: 3, 2: 0, 3: 1}[l] + 7)
                    if l == 1:
                        nc.vector.tensor_scalar(E[:, 0:D], ag, 0.0, None, ALU.min).then_inc(d_el, 1)
                        ch.link(nc.vector.tensor_scalar(ag, ag, 0.0, None, ALU.max))
                        dve.wait_ge(d_ex, t + 1)
                        ch.link(nc.vector.tensor_scalar(E[:, 0:D], E[:, 0:D], 1.0, None, ALU.subtract))
                        ch.link(nc.vector.tensor_tensor(ag, ag, E[:, 0:D], ALU.add))
                    if l == 3:
                        ch.link(nc.vector.tensor_scalar(ag, ag, 0.0, None, ALU.max))
                    xw = E[:, D:2 * D]
                    ch.link(nc.vector.tensor_tensor(xw, xt, ag, ALU.add))
                    ch.link(nc.vector.reduce_sum(small[:, 6:7], xw, AX.X))
                    ch.link(nc.vector.tensor_scalar(small[:, 6:7], small[:, 6:7], 1.0 / D, None, ALU.mult))
                    ch.link(nc.vector.tensor_scalar(xw, xw, small[:, 6:7], None, ALU.subtract))
                    ch.link(nc.vector.tensor_tensor(E[:, 0:D], xw, xw, ALU.mult))
                    ch.link(nc.vector.reduce_sum(small[:, 7:8], E[:, 0:D], AX.X))
                    nc.vector.tensor_scalar(small[:, 8:9], small[:, 7:8], 1.0 / D, EPS, ALU.mult, ALU.add).then_inc(d_var, 1)
                    dve.wait_ge(d_rs, t + (l * T + 1))
                    ch.link(nc.vector.tensor_scalar(xt, xw, small[:, 8:9], None, ALU.mult))
                    ch.endloop(T)
                nc.vector.tensor_copy(small[:, 10:11], small[:, 8:9]).then_inc(d_lay, 1)

        STEPS = T // 2
        TURNS = T // 4
        CONSTS = NC + PACK + 6

        def wait(eng, sem, value):
            if type(value) is not int or value > 0:
                eng.wait_ge(sem, value)

        def of(m, back, pairs=PAIRS):
            return type(m) is not int or 0 <= m - back < pairs

        def tiles(m):
            return slice(2 * m, 2 * m + 2) if type(m) is int else bass.ds(m * 2, 2)

        LAG = 4

        def by_pairs(eng, body, between=lambda: None):
            for m in range(LAG + 2):
                body(m, m % 2)
            with eng.Fori(LAG // 2 + 1, TURNS) as i:
                body(i * 2, 0)
                body(i * 2 + 1, 1)
            for m in range(PAIRS, PAIRS + LAG):
                body(m, m % 2)
                if m == PAIRS:
                    between()

        EARLY = 12

        def scatter(pool, p):
            pool.wait_ge(l_pc, p + 1)
            for t in range(2 * p, 2 * p + 2):
                pool.indirect_dma_start(sorted_rec, bass.IndirectOffsetOnAxis(ap=rank_i[:, t:t + 1], axis=0),
                                        REC[:, t, :], None).then_inc(f_scat, 16)

        def turns(eng, body):
            body(0)
            with eng.Fori(1, TURNS) as i:
                body(i)

        with nc.Block() as block:
            @block.gpsimd
            def _(pool):
                nc.gpsimd.iota(count_f, [[1, WORDS]], base=0, channel_multiplier=-(WORDS // D),
                               allow_small_or_imprecise_dtypes=True).then_inc(s_const, 1)
                nc.gpsimd.iota(first, [[WORDS, PACK]], base=1, channel_multiplier=0,
                               allow_small_or_imprecise_dtypes=True).then_inc(s_const, 1)
                nc.gpsimd.iota(cls, [[-1, NC], [0, T]], base=SLOTS, channel_multiplier=0,
                               allow_small_or_imprecise_dtypes=True).then_inc(s_const, 1)
                for c in range(NC):
                    room = D * sum(r >= SLOTS - c for r in ROOM) if c < SLOTS else N
                    nc.gpsimd.memset(roomy[:, c:c + 1], float(room)).then_inc(s_const, 1)
                nc.gpsimd.memset(strict[:], 1.0).then_inc(s_const, 1)
                nc.gpsimd.memset(wrong, 0.0).then_inc(s_const, 1)
                for b in range(PACK):
                    nc.gpsimd.memset(mask[:, b:b + 1], WORDS << b).then_inc(s_const, 1)
                nc.gpsimd.memset(less_half, -0.5).then_inc(s_const, 1)
                pool.wait_ge(s_const, CONSTS)
                nc.gpsimd.affine_select(out=strict[:], in_=strict[:], compare_op=ALU.is_gt, fill=0.0, base=0,
                                        pattern=[[1, D]], channel_multiplier=-1).then_inc(s_const, 1)
                nc.gpsimd.memset(X0[:, :, D + 1:TW0], 1.0).then_inc(s_const, 1)
                nc.gpsimd.memset(REC[:, :, R_ID + 1:RW], 0.0).then_inc(s_const, 1)
                nc.gpsimd.iota(REC[:, :, R_ID:R_ID + 1], [[D, T], [0, 1]], base=0, channel_multiplier=1,
                               allow_small_or_imprecise_dtypes=True).then_inc(s_const, 1)
                pool.wait_ge(s_const, CONSTS + 4)
                pool.wait_ge(s_arow, 16)
                pool.wait_ge(s_x[3], 16)
                for k in range(2):
                    if k:
                        pool.wait_ge(s_red, 1)
                    nc.gpsimd.tensor_tensor(product, X0[:, quarter(3), 0:D],
                                            a_row[:, 1 - k:2 - k, :].broadcast_to([D, T // 4, D]), ALU.mult).then_inc(s_dot, 1)
                pool.wait_ge(s_tab0, 16 * 4)
                pool.wait_ge(s_row0, 16)

                def gather0(i):
                    for j in range(2):
                        pool.wait_ge(l_idx, i * 2 + (j + 1))
                        wait(pool, l_free, i * 2 + (j - 1))
                        if type(i) is not int:
                            pool.nop(nofuse=True)
                        for t in range(2):
                            for k in range(FEW):
                                pool.indirect_dma_start(G0[j][:, t, k, 0:TW0], None, tables[0],
                                                        bass.IndirectOffsetOnAxis(ap=ix0[j][:, t, k:k + 1], axis=0)).then_inc(l_g[j], 16)

                turns(pool, gather0)
                pool.wait_ge(s_rank, 1)
                for p in range(EARLY):
                    scatter(pool, p)

            @block.sync
            def _(sp):
                sp.wait_ge(s_zrow, 1)
                sp.dma_start(tables[0][0:1, :], row0[0:1, 0:TW0]).then_inc(s_row0, 16)

                def table0():
                    sp.wait_ge(s_const, CONSTS + 4)
                    for c in range(4):
                        sp.wait_ge(s_pjc, c + 1)
                        sp.dma_start(tables[0][1:N + 1, :].rearrange("(t p) w -> p t w", p=D)[:, quarter(c), :],
                                     X0[:, quarter(c), :]).then_inc(s_tab0, 16)

                def turn(m, j):
                    rows = table1_rows(m - LAG) if of(m, LAG) else None
                    for u in range(4):
                        if of(m, -1):
                            source = unit(m + 1, u)
                            sp.wait_ge(s_sign, m * 4 + (u + 1))
                            if type(m) is not int:
                                sp.nop(nofuse=True)
                            sp.wait_ge(s_adj[(u + 2) % 4], m * 16 + (16 if u < 2 else 32))
                            sp.dma_start(ADJ[u], source).then_inc(s_adj[u], 16)
                        if type(m) is int and m == 0 and u == 1:
                            table0()
                    if of(m, LAG):
                        sp.wait_ge(l_pc, m - (LAG - 1))
                        sp.dma_start(rows, stage[j]).then_inc(l_tab[j], 16)

                for m in range(LAG + 2):
                    turn(m, m % 2)
                with sp.Fori(LAG // 2 + 1, TURNS - 1) as i:
                    turn(i * 2, 0)
                    turn(i * 2 + 1, 1)
                for m in range(PAIRS - 2, PAIRS + LAG):
                    turn(m, m % 2)
                sp.wait_ge(l_tab[0], 16 * PAIRS // 2)
                sp.wait_ge(l_tab[1], 16 * PAIRS // 2)

            @block.scalar
            def _(act):
                nc.scalar.preload_act_table_set("natural_log_exp_and_others")
                act.wait_ge(s_const, CONSTS)

                def turn(m, j):
                    q = 1 - j
                    for u in range(4):
                        if of(m, 0):
                            act.wait_ge(s_adj[u], m * 16 + 16)
                            wait(act, s_packed, m * 4 + (u - 1))
                            wait(act, s_dec, m - 1)
                            nc.scalar.activation(SIGN[u % 2], ADJ[u], ACT.Sign, bias=less_half,
                                                 accum_out=degs[:, 4 * j + u:4 * j + u + 1]).then_inc(s_sign, 1)
                        if u == 1 and of(m, 4):
                            act.wait_ge(l_xT, m - 3)
                            nc.scalar.copy(sT[j], psT[j][:, 0:2 * D]).then_inc(l_xTc, 1)
                        if u == 1 and of(m, 3):
                            act.wait_ge(l_e, m - 2)
                            nc.scalar.activation(w0[q], w0[q], ACT.Exp).then_inc(l_w, 1)
                        if u == 3 and of(m, 4):
                            if of(m, 6):
                                act.wait_ge(l_tab[j], 16 * ((m - 6) // 2 + 1) if type(m) is int else m * 8 - (32 + 8 * j))
                            act.wait_ge(l_pr, m - 3)
                            prj = [psA, psB][j][:, 0:2 * WX].rearrange("p (t w) -> p t w", t=2)
                            nc.scalar.copy(REC[:, tiles(m - 4), R_Q1], prj[:, :, QRY])
                            nc.scalar.copy(REC[:, tiles(m - 4), 0:D], x1[j])
                            nc.scalar.copy(stage[j], prj[:, :, 0:TW]).then_inc(l_pc, 1)
                        if u == 3 and of(m, 3):
                            act.wait_ge(l_var, m - 2)
                            nc.scalar.activation(ln0[q], ve0[q], ACT.Ln).then_inc(l_ln, 1)
                            act.wait_ge(l_ln, m - 2)
                            nc.scalar.activation(ve0[q], ln0[q], ACT.Exp, scale=-0.5).then_inc(l_rs, 1)

                by_pairs(act, turn)

            @block.tensor
            def _(pe):
                def transpose0(p):
                    if p % 8 == 0:
                        pe.wait_ge(s_x[p // 8], 16)
                    if p >= 2:
                        pe.wait_ge(s_xzc, p - 1)
                    for t in range(2):
                        last = nc.tensor.transpose(psT[p % 2][:, t * D:(t + 1) * D], X0[:, 2 * p + t, 0:D], ident[:])
                    last.then_inc(s_xz, 1)

                transpose0(0)
                for p in range(PAIRS * 3 // 4):
                    if p + 1 < PAIRS * 3 // 4:
                        transpose0(p + 1)
                    c = p // 8
                    if p % 8 == 0 and c >= 2:
                        pe.wait_ge(s_pjc, c - 1)
                    pe.wait_ge(s_xzc, p + 1)
                    for t in range(2):
                        at = 2 * (2 * (p % 8) + t)
                        last = nc.tensor.matmul([psA, psB][c % 2][:, at:at + 2], sT[p % 2][:, t * D:(t + 1) * D],
                                                Wext[:, 0, KEY:QRY + 1:QRY - KEY], start=True, stop=True)
                    last.then_inc(s_pj, 1)
                pe.wait_ge(s_pconst, 3)

                def pack(m, k):
                    for h in range(2):
                        pe.wait_ge(s_sign, m * 4 + (2 * k + h + 1))
                        if h == 0:
                            wait(pe, s_picked, m * 2 + (k - 1))
                        for c in range(HALF // WORDS):
                            for b in range(WORDS // 512):
                                last = nc.tensor.matmul(PK[k][:, b * 512:(b + 1) * 512], power[:, h * 4 + c, :],
                                                        SIGN[h][:, c * WORDS + b * 512:c * WORDS + (b + 1) * 512],
                                                        start=(h == 0 and c == 0), stop=False)
                        if h == 1:
                            for b in range(WORDS // 512):
                                last = nc.tensor.matmul(PK[k][:, b * 512:(b + 1) * 512], ones_b,
                                                        count_b[:, b * 512:(b + 1) * 512], start=False, stop=True)
                        last.then_inc(s_packed, 1)

                def turn(m, j):
                    if of(m, 0):
                        pack(m, 0)
                    if of(m, 4):
                        pe.wait_ge(l_x, m - 3)
                        if of(m, 6):
                            pe.wait_ge(l_pc, m - 5)
                        for t in range(2):
                            last = nc.tensor.transpose(psT[j][:, t * D:(t + 1) * D], x1[j][:, t, :], ident[:])
                        last.then_inc(l_xT, 1)
                        pe.wait_ge(l_xTc, m - 3)
                        for t in range(2):
                            last = nc.tensor.matmul([psA, psB][j][:, t * WX:(t + 1) * WX], sT[j][:, t * D:(t + 1) * D],
                                                    Wext[:, 1, :], start=True, stop=True)
                        last.then_inc(l_pr, 1)
                    if of(m, 0):
                        pack(m, 1)

                pe.wait_ge(s_pjc, 4)

                def count():
                    pe.wait_ge(s_const, CONSTS + 4)
                    pe.wait_ge(s_cnt, 1)
                    nc.tensor.matmul(psS[:, 0:NC], strict[:], cnt, start=True, stop=True)
                    nc.tensor.matmul(psS[:, 32:32 + NC], ones[:], cnt, start=True, stop=True).then_inc(s_cntm, 1)

                by_pairs(pe, turn, count)
                pe.wait_ge(s_bad, 1)
                nc.tensor.matmul(psS[:, 64:65], ones[:], bad[:, 0:1], start=True, stop=True).then_inc(s_badm, 1)

            @block.vector
            def _(dve):
                ch = Chain(dve, s_fch)
                nc.vector.memset(row0, 0.0).then_inc(s_zrow, 1)
                def constants():
                    dve.wait_ge(s_const, CONSTS)
                    for b in range(PACK):
                        last = nc.vector.tensor_scalar(power[:, b, :], ident[:], float(WORDS // 2 << b), None, ALU.mult)
                    last.then_inc(s_pconst, 1)
                    nc.vector.tensor_copy(ones_b, ones[:]).then_inc(s_pconst, 1)
                    nc.vector.tensor_scalar(count_b, count_f, 0.0, float(WORDS // D), ALU.max, ALU.min).then_inc(s_pconst, 1)

                for p in range(PAIRS * 3 // 4):
                    if p == PAIRS // 2:
                        constants()
                    dve.wait_ge(s_xz, p + 1)
                    if p >= 2:
                        dve.wait_ge(s_pj, p - 1)
                    nc.vector.tensor_copy(sT[p % 2], psT[p % 2][:, 0:2 * D]).then_inc(s_xzc, 1)
                    if p % 8 == 7:
                        c = p // 8
                        dve.wait_ge(s_pj, p + 1)
                        kq = [psA, psB][c % 2][:, 0:T // 2].rearrange("p (t k) -> p t k", k=2)
                        nc.vector.tensor_copy(keys0[:, quarter(c)], kq[:, :, 0])
                        nc.vector.tensor_copy(X0[:, quarter(c), D], kq[:, :, 0])
                        nc.vector.tensor_copy(qrys0[:, quarter(c)], kq[:, :, 1])
                        nc.vector.tensor_copy(REC[:, quarter(c), R_Q0], kq[:, :, 1]).then_inc(s_pjc, 1)
                    if p == PAIRS * 3 // 8:
                        dve.wait_ge(s_dot, 1)
                        ch.link(nc.vector.reduce_sum(keys0[:, quarter(3)], product, AX.X))
                        nc.vector.tensor_copy(X0[:, quarter(3), D], keys0[:, quarter(3)]).then_inc(s_red, 1)
                dve.wait_ge(s_dot, 2)
                ch.link(nc.vector.reduce_sum(qrys0[:, quarter(3)], product, AX.X))
                nc.vector.tensor_copy(REC[:, quarter(3), R_Q0], qrys0[:, quarter(3)]).then_inc(s_pjc, 1)

                def carry():
                    ch.add(nc.vector.memset(small[:, 15:16], 0.0))

                def pick(m, k):
                    dve.wait_ge(s_packed, m * 4 + (2 * k + 2))
                    ch.wait()
                    carry()
                    for g in range(SEGS):
                        last = nc.vector.max(top8[:, k, 8 * g:8 * g + 8], PK[k][:, g * SEG:(g + 1) * SEG])
                    last.then_inc(s_picked, 1)

                def decode(m, j):
                    ds = slice(2 * m, 2 * m + 2) if type(m) is int else bass.ds(m * 2, 2)
                    dve.wait_ge(s_picked, m * 2 + 2)
                    ch.wait()
                    carry()
                    for t in range(2):
                        ch.add(nc.vector.max(word16[:, t, 0:8], top8[:, t, :]))
                    d4 = degs[:, 4 * j:4 * j + 4].rearrange("p (t h) -> p t h", h=2)
                    ch.wait()
                    ch.add(nc.vector.reduce_sum(deg2, d4, AX.X))
                    for t in range(2):
                        ch.add(nc.vector.match_replace(rest8[:, t, :], word16[:, t, 0:8], top8[:, t, :], -1e9))
                    ch.wait()
                    nc.vector.tensor_scalar(deg2, deg2, 0.5, float(HALF), ALU.mult, ALU.add).then_inc(s_dec, 1)
                    for t in range(2):
                        ch.add(nc.vector.max(word16[:, t, 8:16], rest8[:, t, :]))
                    ch.wait()
                    ch.link(nc.vector.tensor_scalar(key16, word16.rearrange("p t s -> p (t s)"), float(SHIFT), None, ALU.add))
                    ch.add(nc.vector.tensor_scalar(col16, key16, WORDS - 1, None, ALU.bitwise_and))
                    shape = [D, 2 * SLOTS, PACK]
                    ch.add(nc.vector.tensor_tensor(bits, key16.unsqueeze(2).broadcast_to(shape), mask.unsqueeze(1).broadcast_to(shape),
                                                   ALU.bitwise_and))
                    ch.wait()
                    ch.link(nc.vector.tensor_tensor(cand, col16.unsqueeze(2).broadcast_to(shape), first.unsqueeze(1).broadcast_to(shape), ALU.add))
                    ch.link(nc.vector.scalar_tensor_tensor(out=cand, in0=bits, scalar=0.0, in1=cand, op0=ALU.is_gt, op1=ALU.mult))
                    carry()
                    per_tile = cand.rearrange("p (t s) b -> p t (s b)", t=2)
                    for t in range(2):
                        ch.add(nc.vector.max(top16[:, t, 0:8], per_tile[:, t, :]))
                    ch.wait()
                    ch.add(nc.vector.tensor_copy(deg[:, ds], deg2))
                    for t in range(2):
                        ch.add(nc.vector.match_replace(rest[:, t, :], top16[:, t, 0:8], per_tile[:, t, :], 0.0))
                    ch.wait()
                    carry()
                    for t in range(2):
                        ch.add(nc.vector.max(top16[:, t, 8:16], rest[:, t, :]))
                    ch.wait()
                    ch.add(nc.vector.tensor_copy(pen0[j], top16[:, :, 0:FEW]))
                    nc.vector.tensor_copy(ix0[j], top16[:, :, 0:FEW]).then_inc(l_idx, 1)
                    ch.add(nc.vector.tensor_copy(REC[:, ds, R_SLOT:R_SLOT + SLOTS], top16))
                    ch.link(nc.vector.tensor_scalar(found, top16, 0.0, None, ALU.is_gt))
                    ch.link(nc.vector.reduce_sum(nfound, found, AX.X))
                    ch.link(nc.vector.tensor_tensor(nfound, nfound, deg2, ALU.not_equal))
                    ch.link(nc.vector.tensor_tensor(wrong, wrong, nfound, ALU.max))

                def score0(m, j):
                    ds = slice(2 * m, 2 * m + 2) if type(m) is int else bass.ds(m * 2, 2)
                    g, w = G0[j], w0[j]
                    row = [D, 2, FEW]
                    ch.wait()
                    ch.add(nc.vector.tensor_scalar(pen0[j], pen0[j], 0.0, None, ALU.is_gt))
                    dve.wait_ge(l_g[j], m * (FEW * 16) + (2 - j) * FEW * 16)
                    ch.wait()
                    ch.add(nc.vector.tensor_tensor(w, g[:, :, :, D], REC[:, ds, R_Q0:R_Q0 + 1].broadcast_to(row), ALU.add))
                    ch.add(nc.vector.tensor_scalar(pen0[j], pen0[j], 1.0, BIG, ALU.subtract, ALU.mult))
                    ch.wait()
                    ch.add(nc.vector.scalar_tensor_tensor(out=w, in0=w, scalar=LAYERS[0][1], in1=w, op0=ALU.mult, op1=ALU.max))
                    ch.link(nc.vector.memset(pen0[j][:, :, 0:1], 0.0))
                    ch.link(nc.vector.tensor_tensor(w, w, pen0[j], ALU.add))
                    ch.link(nc.vector.tensor_reduce(m0, w, AX.X, ALU.max))
                    nc.vector.tensor_tensor(w, w, m0.unsqueeze(2).broadcast_to(row), ALU.subtract).then_inc(l_e, 1)

                def weigh0(m, j):
                    ds = slice(2 * m, 2 * m + 2) if type(m) is int else bass.ds(m * 2, 2)
                    g, w = G0[j], w0[j]
                    dve.wait_ge(l_w, m + 1)
                    ch.link(nc.vector.tensor_reduce(m0, w, AX.X, ALU.add))
                    ch.link(nc.vector.reciprocal(m0, m0))
                    ch.link(nc.vector.tensor_tensor(w, w, m0.unsqueeze(2).broadcast_to([D, 2, FEW]), ALU.mult))
                    v = g[:, :, :, 0:D]
                    ch.link(nc.vector.tensor_tensor(v, v, w.unsqueeze(3).broadcast_to([D, 2, FEW, D]), ALU.mult))
                    wait(dve, l_pc, m - 1)
                    nc.vector.tensor_reduce(ag0, v.rearrange("p t s d -> p t d s"), AX.X, ALU.add).then_inc(l_free, 1)
                    dve.wait_ge(l_free, m + 1)
                    ch.link(nc.vector.tensor_tensor(x1[j], ag0, X0[:, ds, 0:D], ALU.add))
                    for t in range(2):
                        ch.add(nc.vector.bn_stats(st0[:, t, :], x1[j][:, t, :]))
                    ch.wait()
                    carry()
                    for t in range(2):
                        ch.add(nc.vector.bn_aggr(mv0[j][:, t, :], st0[:, t, :]))
                    ch.wait()
                    nc.vector.tensor_scalar(ve0[j], mv0[j][:, :, 1], EPS, None, ALU.add).then_inc(l_var, 1)

                def norm0(m, j):
                    dve.wait_ge(l_rs, m + 1)
                    for t in range(2):
                        last = nc.vector.tensor_scalar(x1[j][:, t, :], x1[j][:, t, :], mv0[j][:, t, 0:1], ve0[j][:, t:t + 1],
                                                       ALU.subtract, ALU.mult)
                    last.then_inc(l_x, 1)

                def turn(m, j):
                    q = 1 - j
                    if of(m, 1):
                        pick(m - 1, 1)
                    if of(m, 4):
                        norm0(m - 4, j)
                    if of(m, 3):
                        score0(m - 3, q)
                    if of(m, 1):
                        decode(m - 1, q)
                    if of(m, 0):
                        pick(m, 0)
                    if of(m, 3):
                        weigh0(m - 3, q)

                for m in range(LAG + 2):
                    if m == LAG:
                        before = ch.count
                    turn(m, m % 2)
                PER = ch.count - before
                with dve.Fori(LAG // 2 + 1, TURNS) as i:
                    ch.loop(i - (LAG // 2 + 1), PER)
                    turn(i * 2, 0)
                    turn(i * 2 + 1, 1)
                    ch.endloop(TURNS - (LAG // 2 + 1))
                turn(PAIRS, 0)
                ch.link(nc.vector.tensor_scalar(run[:, 0, :], deg, float(SLOTS), None, ALU.min))
                ch.link(nc.vector.tensor_tensor(ind, cls, run[:, 0:1, :].broadcast_to([D, NC, T]), ALU.is_equal))
                flat = "p c t -> p (c t)"
                ch.link(nc.vector.tensor_tensor_scan(run.rearrange(flat), ind.rearrange(flat), ind.rearrange(flat), 0.0, ALU.add, ALU.max))
                nc.vector.reduce_sum(cnt, ind, AX.X).then_inc(s_cnt, 1)
                dve.wait_ge(s_cntm, 1)
                ch.link(nc.vector.tensor_copy(tot, psS[:, 32:32 + NC]))
                ch.link(nc.vector.tensor_tensor_scan(off, tot, tot, 0.0, ALU.add, ALU.max))
                ch.link(nc.vector.tensor_tensor(cls[:, 0, 0:NC], off, roomy, ALU.is_gt))
                ch.link(nc.vector.tensor_copy(cls[:, 1, 0:1], off[:, SLOTS - 1:SLOTS]))
                ch.link(nc.vector.tensor_tensor(off, off, tot, ALU.subtract))
                ch.link(nc.vector.tensor_tensor(off, off, psS[:, 0:NC], ALU.add))
                ch.link(nc.vector.tensor_tensor(off, off, run[:, :, T - 1], ALU.subtract))
                ch.link(nc.vector.tensor_tensor(off, off, cnt, ALU.add))
                ch.link(nc.vector.tensor_tensor(run, run, off.unsqueeze(2).broadcast_to([D, NC, T]), ALU.add))
                ch.link(nc.vector.tensor_tensor(run, run, ind, ALU.mult))
                ch.link(nc.vector.reduce_sum(rank1[:], run.rearrange("p c t -> p t c"), AX.X))
                nc.vector.tensor_copy(rank_i[:], rank1[:]).then_inc(s_rank, 1)
                for m in range(PAIRS + 1, PAIRS + LAG + 1):
                    turn(m, m % 2)

                ch.link(nc.vector.reduce_max(small[:, 0:1], cls[:, 0, 0:NC], AX.X))
                ch.link(nc.vector.reduce_max(small[:, 1:2], wrong, AX.X))
                ch.link(nc.vector.reduce_max(small[:, 2:3], deg, AX.X))
                ch.link(nc.vector.tensor_scalar(small[:, 2:3], small[:, 2:3], SLOTS + 0.5, None, ALU.is_gt))
                ch.link(nc.vector.tensor_scalar(small[:, 3:4], cls[:, 1, 0:1], N - 2 * D - 0.5, None, ALU.is_lt))
                ch.link(nc.vector.reduce_max(small[:, 4:5], small[:, 0:4], AX.X))
                nc.vector.tensor_scalar(bad[:, 0:1], small[:, 4:5], 0.0, 1.0 / D, ALU.is_gt, ALU.mult).then_inc(s_bad, 1)
                dve.wait_ge(s_badm, 1)
                if FORCE == "dense":
                    ch.link(nc.vector.memset(bad_i[:], 1))
                else:
                    ch.link(nc.vector.tensor_scalar(bad_i[:], psS[:, 64:65], 0.0, None, ALU.is_gt))

        def room(p):
            return ROOM[2 * p] + ROOM[2 * p + 1]

        def groups(p):
            return [(0, 2)] if ROOM[2 * p] == ROOM[2 * p + 1] else [(0, 1), (1, 2)]

        def part(buffer, p, a, b, w):
            S = ROOM[2 * p + a]
            at = a * ROOM[2 * p] * w
            return buffer[:, at:at + (b - a) * S * w].rearrange("p (t s w) -> p t s w", t=b - a, w=w)

        def buf(n, p, a, b):
            return part(G[n % NB], p, a, b, TW)

        def wts(n, p, heads, a, b):
            return part(WT4[n % NB], p, a, b, heads)

        SEQ = [PAIRS // 2] + [p for k in range(PAIRS // 2 - 1) for p in (PAIRS - 1 - k, k)] + [PAIRS // 2 - 1]
        ORDER = [(0, PAIRS - 1), (0, 0)] + [(l, p) for l in (1, 2, 3) for p in SEQ]
        NUM = {lp: n for n, lp in enumerate(ORDER)}
        total_g = [0] * NB
        reach = {}
        for n, (l, p) in enumerate(ORDER):
            assert n % NB < 3 or room(p) <= SLOTS
            total_g[n % NB] += (room(p) + (2 if l in (0, 3) else 0)) * 16
            reach[n] = total_g[n % NB]

        def fast_gpsimd(pool):
            nc.gpsimd.iota(place_n, [[1, 2 * D]], base=N - 2 * D + 1, channel_multiplier=0,
                           allow_small_or_imprecise_dtypes=True).then_inc(f_fconst, 1)
            for e, at in enumerate((N - 2 * D + 1, 1)):
                nc.gpsimd.iota(ends[:, e, :, :], [[D, 2], [0, 3]], base=at, channel_multiplier=1,
                               allow_small_or_imprecise_dtypes=True).then_inc(f_fconst, 1)
            for p in range(EARLY, PAIRS):
                scatter(pool, p)

            def own(p):
                for t in range(2 * p, 2 * p + 2):
                    pool.indirect_dma_start(SX[:, t, 0:D + 1], None, rows3,
                                            bass.IndirectOffsetOnAxis(ap=RID[:, t:t + 1], axis=0)).then_inc(f_g[NUM[3, p] % NB], 16)

            def gather(l, p):
                n = NUM[l, p]
                if n >= NB:
                    pool.wait_ge(f_gfree, n - NB + 1)
                if l == 3 and p not in SEQ[:NB]:
                    own(p)
                for t in range(2):
                    for k in range(ROOM[2 * p + t]):
                        pool.indirect_dma_start(buf(n, p, t, t + 1)[:, 0, k, 0:TW if l else TW0], None, tables[l],
                                                bass.IndirectOffsetOnAxis(ap=(IDX if l == 2 else IDN)[:, 2 * p + t, k:k + 1], axis=0)).then_inc(f_g[n % NB], 16)

            pool.wait_ge(f_idx, 1)
            for p in (PAIRS - 1, 0):
                for t in range(2 * p, 2 * p + 2):
                    pool.indirect_dma_start(SX[:, t, 0:D], None, x,
                                            bass.IndirectOffsetOnAxis(ap=RID[:, t:t + 1], axis=0)).then_inc(f_g[NUM[0, p] % NB], 16)
                gather(0, p)
            pool.wait_ge(f_rank, 16)
            for e in range(2):
                pool.wait_ge(f_pc, e + 1)
                for t in range(2):
                    pool.indirect_dma_start(tables[1], bass.IndirectOffsetOnAxis(ap=RID1[:, 2 * e + t:2 * e + t + 1], axis=0),
                                            stage[e][:, t, :], None).then_inc(f_fix[e], 16)
            for l in (1, 2):
                if l == 1:
                    pool.wait_ge(f_idx, 2)
                    pool.wait_ge(f_fix[0], 32)
                    pool.wait_ge(f_fix[1], 32)
                else:
                    for k in range(NS):
                        pool.wait_ge(f_tab[k], 16 * PAIRS // NS)
                pool.wait_ge(f_tab0, 16 * l)
                for p in SEQ:
                    gather(l, p)
            for i, p in enumerate(SEQ):
                pool.wait_ge(f_agg2, i + 1)
                for t in range(2 * p, 2 * p + 2):
                    pool.indirect_dma_start(layer2_nat, bass.IndirectOffsetOnAxis(ap=RID[:, t:t + 1], axis=0),
                                            SX[:, t, 0:2 * D], None).then_inc(f_nat, 16)
            for i in range(PAIRS):
                pool.wait_ge(f_natl[i // 8], 16 * 8)
                p = natural(SEQ[i])
                h, b = 2 * p // 16, 2 * p % 16
                for t in range(2):
                    xk = XN[:, 2 * p + t, 0:D].rearrange("p (k d) -> p k d", k=4)
                    last = nc.gpsimd.tensor_tensor(xk, xk, AGL[:, b + t, :, 32 * h:32 * h + 32], ALU.add)
                last.then_inc(f_added, 1)
            pool.wait_ge(f_xq, 16 * PAIRS)
            for p in SEQ[:NB]:
                own(p)
            for k in range(NS):
                pool.wait_ge(f_tab[k], 16 * 2 * PAIRS // NS)
            pool.wait_ge(f_tab0, 16 * 3)
            for i, p in enumerate(SEQ):
                gather(3, p)
                if i >= 4:
                    store(pool, SEQ[i - 4])
            for p in SEQ[-4:]:
                store(pool, p)
            pool.wait_ge(f_out, 16 * T)

        def store(pool, p):
            pool.wait_ge(f_x, NUM[3, p] + 1)
            for t in range(2 * p, 2 * p + 2):
                pool.indirect_dma_start(out, bass.IndirectOffsetOnAxis(ap=RID[:, t:t + 1], axis=0),
                                        SX[:, t, 0:D], None).then_inc(f_out, 16)

        def natural(p):
            i = SEQ.index(p)
            return 8 * (i % 8 // 2) + 2 * (i // 8) + i % 2

        def table_rows(l, p):
            return tables[l][1 + 2 * p * D:1 + 2 * (p + 1) * D, :].rearrange("(t p) w -> p t w", p=D)

        def fast_sync(sp):
            with nc.allow_non_contiguous_dma(reason="one column"):
                sp.dma_start(tables[1][1:N + 1, KEY + 1:KEY + 2].rearrange("(t p) w -> p t w", p=D),
                             rank1[:].unsqueeze(2)).then_inc(f_rank, 16)
            sp.wait_ge(f_scat, 16 * T)
            in_order = sorted_rec[1:N + 1, :].rearrange("(t p) w -> p t w", p=D)
            for t in (0, T - 2):
                sp.dma_start(SX[:, t:t + 2, 0:RW], in_order[:, t:t + 2, :]).then_inc(f_rec, 16)
            sp.dma_start(SX[:, 2:T - 2, 0:RW], in_order[:, 2:T - 2, :]).then_inc(f_rest, 16)
            sp.wait_ge(f_row0, 1)
            sp.dma_start(tables[1][0:1, :], row0[0:1, :]).then_inc(f_tab0, 16)
            for l in (2, 3):
                for i in range(PAIRS):
                    n = NUM[l - 1, SEQ[i]]
                    sp.wait_ge(f_pc, n + 1)
                    p = natural(SEQ[i]) if l == 3 else SEQ[i]
                    sp.dma_start(table_rows(l, p), stage[n % NS]).then_inc(f_tab[n % NS], 16)
                    if l == 3:
                        sp.dma_start(rows3[2 * p * D:2 * (p + 1) * D, :].rearrange("(t p) w -> p t w", p=D),
                                     XN[:, 2 * p:2 * p + 2, :]).then_inc(f_xq, 16)
                sp.wait_ge(f_row0, l)
                sp.dma_start(tables[l][0:1, :], row0[0:1, :]).then_inc(f_tab0, 16)

        def fast_scalar(act):
            def load_natural():
                act.wait_ge(f_nat, 16 * T)
                by_four = layer2_nat.rearrange("(b p k) w -> k p b w", p=D, k=4)
                by_node = layer2_nat[:, 0:D].rearrange("(t p) d -> p t d", p=D)
                for c in range(4):
                    for k in range(4):
                        act.dma_start(AGL[:, 4 * c:4 * c + 4, k, :], by_four[k, :, 4 * c:4 * c + 4, D:2 * D]).then_inc(f_natl[c], 16)
                        t = 16 * k + 4 * c
                        act.dma_start(XN[:, t:t + 4, 0:D], by_node[:, t:t + 4, :]).then_inc(f_natl[c], 16)

            def iso_sum(c):
                act.wait_ge(f_qb, 3)
                if c >= 4:
                    act.wait_ge(f_im, c - 3)
                for j in range(4):
                    last = nc.scalar.activation(EE[:, c % 4, j * 2 * D:(j + 1) * 2 * D], QB[:, 0:2 * D], ACT.Identity,
                                                bias=keys0[:, 4 * c + j:4 * c + j + 1])
                last.then_inc(f_ia, 1)

            def iso(c):
                act.wait_ge(f_ie, c + 1)
                nc.scalar.activation(EE[:, c % 4, :], EE[:, c % 4, :], ACT.Exp).then_inc(f_ip, 1)

            def exp_w(l, p):
                n = NUM[l, p]
                act.wait_ge(f_e, n + 1)
                w = WT4[n % NB][:, 0:room(p) * LAYERS[l][0]]
                nc.scalar.activation(w, w, ACT.Exp).then_inc(f_w, 1)

            def elu(p):
                n = NUM[1, p]
                act.wait_ge(f_t, n - 1)
                nc.scalar.activation(UE[n % 2], UE[n % 2], ACT.Exp).then_inc(f_u, 1)

            def rstd(m):
                act.wait_ge(f_var, m + 1)
                nc.scalar.activation(lnv[m % NB], mv[m % NB][:, :, 1], ACT.Ln, bias=eps_col).then_inc(f_ln, 1)
                act.wait_ge(f_ln, m + 1)
                nc.scalar.activation(ve[m % NB], lnv[m % NB], ACT.Exp, scale=-0.5).then_inc(f_rs, 1)

            def copy_T(l, p):
                n = NUM[l - 1, p]
                act.wait_ge(f_xT, n + 1)
                if n >= 2:
                    act.wait_ge(f_pr, n - 1)
                if l == 3:
                    i = SEQ.index(p)
                    nc.scalar.activation(sT[n % 2], psT[n % 2][:, 0:2 * D], ACT.Copy, accum_out=x_sums[:, i:i + 1]).then_inc(f_xTc, 1)
                else:
                    nc.scalar.copy(sT[n % 2], psT[n % 2][:, 0:2 * D]).then_inc(f_xTc, 1)

            def stage_out(l, p):
                n = NUM[l - 1, p]
                act.wait_ge(f_pr, n + 1)
                if n in (NS, NS + 1):
                    act.wait_ge(f_fix[n - NS], 32)
                if n >= NS + 2:
                    act.wait_ge(f_tab[n % NS], 16 * ((n - 2) // NS))
                    act.wait_ge(f_mn, min(n - NS - 1, PAIRS))
                prj = [psA, psB][n % 2][:, 0:2 * WX].rearrange("p (t w) -> p t w", t=2)
                if l == 3:
                    at = 2 * natural(p)
                    nc.scalar.copy(XN[:, at:at + 2, D:D + 1], prj[:, :, QRY:QRY + 1])
                else:
                    nc.scalar.copy(QS[:, 2 * p:2 * p + 2, :], prj[:, :, QRY:WX])
                if l == 1:
                    act.wait_ge(f_fconst, 3)
                    nc.scalar.copy(stage[n][:, :, D + 1:TW], ends[:, n, :, :])
                    nc.scalar.copy(stage[n][:, :, 0:D + 1], prj[:, :, 0:D + 1]).then_inc(f_pc, 1)
                else:
                    nc.scalar.copy(stage[n % NS], prj[:, :, 0:TW]).then_inc(f_pc, 1)

            def mean(l):
                act.wait_ge(f_mn, PAIRS + l - 2)
                act.wait_ge(f_tab0, 16 * (l - 1))
                nc.scalar.activation(row0[0:1, :], acc[0:1, 0:TW], ACT.Copy, scale=1.0 / N).then_inc(f_row0, 1)

            for c in range(3):
                iso_sum(c)
            for c in range(T // 4):
                iso(c)
                if c + 3 < T // 4:
                    iso_sum(c + 3)
            act.wait_ge(f_idx, 2)
            for p in (PAIRS - 1, 0):
                exp_w(0, p)
                rstd(NUM[0, p])
                copy_T(1, p)
                stage_out(1, p)
            act.wait_ge(f_cs, 1)
            nc.scalar.copy(sum_row[0:1, :], acc[0:1, 300:300 + D]).then_inc(f_csc, 1)
            act.wait_ge(f_cs, 2)
            nc.scalar.copy(csum, acc[:, 300:301]).then_inc(f_csc, 1)
            act.wait_ge(f_cs, 3)
            nc.scalar.activation(row0[0:1, :], acc[0:1, 0:TW], ACT.Copy, scale=1.0 / N).then_inc(f_row0, 1)
            for l in (1, 2, 3):
                for q in range(PAIRS + 1):
                    if q < PAIRS:
                        exp_w(l, SEQ[q])
                    if l == 1 and q >= 1:
                        copy_T(2, SEQ[q - 1])
                        stage_out(2, SEQ[q - 1])
                    if q < PAIRS:
                        if l == 1:
                            elu(SEQ[q])
                        if l != 2:
                            rstd(NUM[l, SEQ[q]])
                if l == 1:
                    mean(2)
                if l == 2:
                    load_natural()
                    for q in range(PAIRS + 2):
                        if q < PAIRS:
                            rstd(NUM[2, SEQ[q]])
                        if 1 <= q <= PAIRS:
                            copy_T(3, SEQ[q - 1])
                        if q >= 2:
                            stage_out(3, SEQ[q - 2])
                    mean(3)

        def fast_tensor(pe):
            for t in range(T):
                pe.wait_ge(f_oh, t + 1)
                for h in range(2):
                    last = nc.tensor.matmul([psS, psT1][h][:, 0:3], MARK[:, t % 8, h * D:(h + 1) * D], q_part[:, :, t],
                                            start=(t == 0), stop=(t == T - 1))
                last.then_inc(f_ohm, 1)
            pe.wait_ge(f_qb, 2)
            nc.tensor.matmul(psS[:, 0:2 * D], ones[:], EE[:, 0, 0:2 * D], start=True, stop=True).then_inc(f_ohm, 1)
            pe.wait_ge(f_kd, 1)
            nc.tensor.matmul(psB[0:1, 0:D], small[:, 0:1], ident[:], start=True, stop=True).then_inc(f_km, 1)
            pe.wait_ge(f_kd, 2)
            nc.tensor.matmul(psB[:, D:D + 1], ones[0:1, :], small[0:1, 1:2], start=True, stop=True).then_inc(f_km, 1)

            def iso(c):
                pe.wait_ge(f_ip, c + 1)
                for j in range(4 * c, 4 * c + 4):
                    for t in range(2):
                        e = EE[:, c % 4, (j % 4) * 2 * D + t * D:(j % 4) * 2 * D + (t + 1) * D]
                        last = nc.tensor.matmul(psD[t][:, 0:TW0], e, X0[:, j, :], start=(j == 0), stop=(j == T - 1))
                last.then_inc(f_im, 1)

            def transpose(l, p):
                n = NUM[l - 1, p]
                pe.wait_ge(f_x, n + 1)
                if n >= 2:
                    pe.wait_ge(f_xTc, n - 1)
                for t in range(2):
                    src = XN[:, 2 * natural(p) + t, 0:D] if l == 3 else SX[:, 2 * p + t, 0:D]
                    last = nc.tensor.transpose(psT[n % 2][:, t * D:(t + 1) * D], src, ident[:])
                last.then_inc(f_xT, 1)

            def project(l, p):
                n = NUM[l - 1, p]
                pe.wait_ge(f_xTc, n + 1)
                if n >= 2:
                    pe.wait_ge(f_pc, n - 1)
                for t in range(2):
                    last = nc.tensor.matmul([psA, psB][n % 2][:, t * WX:(t + 1) * WX], sT[n % 2][:, t * D:(t + 1) * D],
                                            Wext[:, l, :], start=True, stop=True)
                last.then_inc(f_pr, 1)

            def average(l, p):
                n = NUM[l - 1, p]
                pe.wait_ge(f_pc, n + 1)
                if p == SEQ[0]:
                    pe.wait_ge(f_row0, l - 1)
                for t in range(2):
                    last = nc.tensor.matmul(acc[0:1, 0:TW], ones[:, 0:1], stage[n % NS][:, t, :],
                                            start=(p == SEQ[0] and t == 0), stop=(p == SEQ[-1] and t == 1))
                last.then_inc(f_mn, 1)

            for c in range(T // 4):
                iso(c)
            def sum_pair(p):
                for t in range(2 * p, 2 * p + 2):
                    last = nc.tensor.matmul(acc[0:1, 300:300 + D], ones[:, 0:1], SX[:, t, 0:D], start=(t == 2), stop=(t == 1))
                return last

            pe.wait_ge(f_rest, 16)
            for p in range(1, PAIRS // 2):
                sum_pair(p)
            transpose(1, PAIRS - 1)
            project(1, PAIRS - 1)
            for p in range(PAIRS // 2, PAIRS):
                sum_pair(p)
            transpose(1, 0)
            project(1, 0)
            last = sum_pair(0)
            last.then_inc(f_cs, 1)
            pe.wait_ge(f_csc, 1)
            nc.tensor.matmul(acc[:, 300:301], sum_row[0:1, :], ones[0:1, 0:1], start=True, stop=True).then_inc(f_cs, 1)
            pe.wait_ge(f_csc, 2)
            nc.tensor.matmul(acc[0:1, 0:TW], csum, Wext[:, 1, 0:TW], start=True, stop=True).then_inc(f_cs, 1)
            for p in SEQ:
                transpose(2, p)
                project(2, p)
                average(2, p)
            for q in range(PAIRS + 1):
                if q < PAIRS:
                    transpose(3, SEQ[q])
                if q >= 1:
                    project(3, SEQ[q - 1])
            pe.wait_ge(f_cs, 4)
            pe.wait_ge(f_row0, 2)
            nc.tensor.matmul(acc[0:1, 0:TW], csum, Wext[:, 3, 0:TW], start=True, stop=True).then_inc(f_mn, 1)

        def fast_vector(dve):
            ch = Chain(dve, f_ch)
            ch.add(nc.vector.memset(eps_col, EPS))
            dve.wait_ge(f_fconst, 3)
            rest_of = qrys0[:]
            for k in range(3):
                ch.link(nc.vector.tensor_copy(q_part[:, k, :], rest_of))
                if k < 2:
                    ch.link(nc.vector.tensor_tensor(q_rest, rest_of, q_part[:, k, :], ALU.subtract))
                    rest_of = q_rest
            for t in range(T):
                if t >= 8:
                    dve.wait_ge(f_ohm, t - 7)
                nc.vector.tensor_scalar(MARK[:, t % 8, :], place_n, rank1[:, t:t + 1], None, ALU.is_equal).then_inc(f_oh, 1)
            nc.vector.reduce_max(small[:, 0:1], keys0[:], AX.X).then_inc(f_kd, 1)
            dve.wait_ge(f_ohm, T)
            ch.add(nc.vector.reduce_sum(q_col[:, 0:1], psS[:, 0:3], AX.X))
            ch.link(nc.vector.reduce_sum(q_col[:, 1:2], psT1[:, 0:3], AX.X))
            for h in range(2):
                nc.vector.tensor_scalar(EE[:, 0, h * D:(h + 1) * D], ident[:], q_col[:, h:h + 1], None, ALU.mult).then_inc(f_qb, 1)
            dve.wait_ge(f_km, 1)
            nc.vector.reduce_max(small[0:1, 1:2], psB[0:1, 0:D], AX.X).then_inc(f_kd, 1)
            slope, neg = LAYERS[0][1], LAYERS[0][2]
            dve.wait_ge(f_ohm, T + 1)
            nc.vector.tensor_copy(QB[:, 0:2 * D], psS[:, 0:2 * D]).then_inc(f_qb, 1)
            dve.wait_ge(f_km, 2)
            ch.link(nc.vector.tensor_copy(small[:, 2:3], psB[:, D:D + 1]))
            dve.wait_ge(f_qb, 3)
            MB = QB[:, 2 * D:4 * D]
            ch.link(nc.vector.tensor_scalar(MB, QB[:, 0:2 * D], small[:, 2:3], None, ALU.add))
            ch.link(nc.vector.scalar_tensor_tensor(out=MB, in0=MB, scalar=slope, in1=MB, op0=ALU.mult, op1=ALU.max))
            ch.link(nc.vector.tensor_scalar(MB, MB, neg, None, ALU.add))

            def iso_slope(c):
                dve.wait_ge(f_ia, c + 1)
                e = EE[:, c % 4, :]
                nc.vector.scalar_tensor_tensor(out=e, in0=e, scalar=slope, in1=e, op0=ALU.mult, op1=ALU.max).then_inc(f_il, 1)

            def iso(c):
                dve.wait_ge(f_il, c + 1)
                e3 = EE[:, c % 4, :].rearrange("p (j i) -> p j i", j=4)
                nc.vector.scalar_tensor_tensor(out=e3, in0=e3, scalar=neg, in1=QB[:, 2 * D:4 * D].unsqueeze(1).broadcast_to([D, 4, 2 * D]),
                                               op0=ALU.add, op1=ALU.subtract).then_inc(f_ie, 1)

            slots = SX[:, :, R_SLOT:R_SLOT + SLOTS]

            def ids(a, b):
                ch.add(nc.vector.tensor_copy(RID[:, a:b], SX[:, a:b, R_ID]))
                ch.add(nc.vector.tensor_copy(IDN[:, a:b, :], slots[:, a:b, :]))

            def penalties(a, b, query):
                ch.add(nc.vector.tensor_copy(QS[:, a:b, 0], SX[:, a:b, query]))
                ch.link(nc.vector.tensor_scalar(PEN[:, a:b, :], slots[:, a:b, :], 0.0, None, ALU.is_gt))
                ch.link(nc.vector.tensor_scalar(PEN[:, a:b, :], PEN[:, a:b, :], 1.0, BIG, ALU.subtract, ALU.mult))
                ch.link(nc.vector.memset(PEN[:, a:b, 0:1], 0.0))

            def end_records():
                dve.wait_ge(f_rec, 32)
                ids(0, 2)
                ids(T - 2, T)
                ch.add(nc.vector.tensor_scalar(RID1[:, 0:2], SX[:, T - 2:T, R_ID], 1.0, None, ALU.add))
                ch.wait()
                nc.vector.tensor_scalar(RID1[:, 2:4], SX[:, 0:2, R_ID], 1.0, None, ALU.add).then_inc(f_idx, 1)

            iso_slope(0)
            for c in range(T // 4):
                if c + 1 < T // 4:
                    iso_slope(c + 1)
                iso(c)
                if c == 7:
                    end_records()
            penalties(0, 2, R_Q0)
            penalties(T - 2, T, R_Q0)
            ch.link(nc.vector.tensor_scalar(ISO, SX[:, T - 2:T, R_SLOT], 0.0, None, ALU.is_equal))
            dve.wait_ge(f_im, T // 4)
            for t in range(2):
                ch.add(nc.vector.reciprocal(small[:, 8 + t:9 + t], psD[t][:, D + 1:TW0]))
            ch.wait()
            for t in range(2):
                ch.add(nc.vector.tensor_scalar(UE[0][:, t, :], psD[t][:, 0:D], small[:, 8 + t:9 + t], None, ALU.mult))
            dve.wait_ge(f_rest, 16)
            ids(2, T - 2)
            penalties(2, T - 2, R_Q1)
            dve.wait_ge(f_idx, 1)
            nc.vector.tensor_copy(small[:, 10:11], small[:, 2:3]).then_inc(f_idx, 1)

            def score(l, p):
                heads, slope, _ = LAYERS[l]
                n = NUM[l, p]
                dve.wait_ge(f_g[n % NB], reach[n])
                m = mx[n % NB][:, 0:2 * heads].rearrange("p (t h) -> p t h", t=2)
                for t in range(2):
                    g, w = buf(n, p, t, t + 1)[:, 0], wts(n, p, heads, t, t + 1)[:, 0]
                    q = QS[:, 2 * p + t, 0:heads] if l < 3 else SX[:, 2 * p + t, D:D + 1]
                    last = nc.vector.tensor_tensor(w, g[:, :, D:D + heads], q.unsqueeze(1).broadcast_to(w.shape), ALU.add)
                ch.link(last)
                flat = WT4[n % NB][:, 0:room(p) * heads]
                ch.link(nc.vector.scalar_tensor_tensor(out=flat, in0=flat, scalar=slope, in1=flat, op0=ALU.mult, op1=ALU.max))
                if ROOM[2 * p] > 1:
                    for t in range(2):
                        w = wts(n, p, heads, t, t + 1)[:, 0]
                        last = nc.vector.tensor_tensor(w, w, PEN[:, 2 * p + t, 0:w.shape[1]].unsqueeze(2).broadcast_to(w.shape), ALU.add)
                    ch.link(last)
                for a, b in groups(p):
                    last = nc.vector.tensor_reduce(m[:, a:b, :], wts(n, p, heads, a, b).rearrange("p t s h -> p t h s"), AX.X, ALU.max)
                ch.link(last)
                for t in range(2):
                    w = wts(n, p, heads, t, t + 1)[:, 0]
                    last = nc.vector.tensor_tensor(w, w, m[:, t, :].unsqueeze(1).broadcast_to(w.shape), ALU.subtract)
                last.then_inc(f_e, 1)

            def weigh(l, p):
                heads = LAYERS[l][0]
                n = NUM[l, p]
                dve.wait_ge(f_w, n + 1)
                m = mx[n % NB][:, 0:2 * heads].rearrange("p (t h) -> p t h", t=2)
                for a, b in groups(p):
                    last = nc.vector.tensor_reduce(m[:, a:b, :], wts(n, p, heads, a, b).rearrange("p t s h -> p t h s"), AX.X, ALU.add)
                ch.link(last)
                ch.link(nc.vector.reciprocal(m, m))
                for t in range(2):
                    w = wts(n, p, heads, t, t + 1)[:, 0]
                    last = nc.vector.tensor_tensor(w, w, m[:, t, :].unsqueeze(1).broadcast_to(w.shape), ALU.mult)
                ch.link(last)
                if l == 1:
                    for a, b in groups(p):
                        nc.vector.tensor_copy(IDX[:, 2 * p + a:2 * p + b, 0:ROOM[2 * p + a]], buf(n, p, a, b)[:, :, :, D + 1])
                for t in range(2):
                    v = buf(n, p, t, t + 1)[:, 0, :, 0:D].rearrange("p s (h d) -> p s h d", h=heads)
                    last = nc.vector.tensor_tensor(v, v, wts(n, p, heads, t, t + 1)[:, 0].unsqueeze(3).broadcast_to(v.shape), ALU.mult)
                ch.link(last)
                dst = SX[:, 2 * p:2 * p + 2, D:2 * D] if l == 2 else AGP[n % NB]
                for a, b in groups(p):
                    last = nc.vector.tensor_reduce(dst[:, a:b, :], buf(n, p, a, b)[:, :, :, 0:D].rearrange("p t s d -> p t d s"), AX.X, ALU.add)
                last.then_inc(f_gfree, 1)
                dve.wait_ge(f_gfree, n + 1)
                if l == 0 and p == PAIRS - 1:
                    ch.link(nc.vector.tensor_tensor(UE[0], UE[0], dst, ALU.subtract))
                    for t in range(2):
                        ch.add(nc.vector.scalar_tensor_tensor(out=dst[:, t, :], in0=UE[0][:, t, :], scalar=ISO[:, t:t + 1],
                                                              in1=dst[:, t, :], op0=ALU.mult, op1=ALU.add))
                    ch.wait()
                if l == 1:
                    nc.vector.tensor_scalar(UE[n % 2], dst, 0.0, None, ALU.min).then_inc(f_t, 1)
                if l == 2:
                    nc.vector.tensor_copy(small[:, 9:10], SX[:, 2 * p + 1, 2 * D - 1:2 * D]).then_inc(f_agg2, 1)

            def residual(l, p, between=None):
                n = m = NUM[l, p]
                if l == 2:
                    dve.wait_ge(f_added, SEQ.index(p) + 1)
                    xp = XN[:, 2 * natural(p):2 * natural(p) + 2, 0:D]
                else:
                    xp = SX[:, 2 * p:2 * p + 2, 0:D]
                    ag = AGP[n % NB]
                    if l == 0:
                        ch.link(nc.vector.tensor_tensor(xp, xp, ag, ALU.add))
                    else:
                        ch.link(nc.vector.scalar_tensor_tensor(out=xp, in0=ag, scalar=0.0, in1=xp, op0=ALU.max, op1=ALU.add))
                    if l == 1:
                        dve.wait_ge(f_u, n - 1)
                        ch.link(nc.vector.scalar_tensor_tensor(out=xp, in0=UE[n % 2], scalar=-1.0, in1=xp, op0=ALU.add, op1=ALU.add))
                for t in range(2):
                    last = nc.vector.bn_stats(st6[m % 2][:, t, :], xp[:, t, :])
                ch.add(last)
                if between:
                    between()
                ch.wait()
                for t in range(2):
                    last = nc.vector.bn_aggr(mv[m % NB][:, t, :], st6[m % 2][:, t, :])
                last.then_inc(f_var, 1)

            def norm(l, p):
                m = NUM[l, p]
                dve.wait_ge(f_rs, m + 1)
                xp = XN[:, 2 * natural(p):2 * natural(p) + 2, 0:D] if l == 2 else SX[:, 2 * p:2 * p + 2, 0:D]
                for t in range(2):
                    last = nc.vector.tensor_scalar(xp[:, t, :], xp[:, t, :], mv[m % NB][:, t, 0:1], ve[m % NB][:, t:t + 1],
                                                   ALU.subtract, ALU.mult)
                last.then_inc(f_x, 1)

            for p in (PAIRS - 1, 0):
                score(0, p)
                weigh(0, p)
                residual(0, p)
                norm(0, p)
            dve.wait_ge(f_pc, 2)
            for l in (1, 2, 3):
                for q in range(PAIRS + 1):
                    if q < PAIRS:
                        score(l, SEQ[q])
                    if l != 2 and q >= 1:
                        norm(l, SEQ[q - 1])
                    if q < PAIRS:
                        weigh(l, SEQ[q])
                        if l != 2:
                            residual(l, SEQ[q])
                if l == 2:
                    residual(2, SEQ[0])
                    for q in range(1, PAIRS):
                        residual(2, SEQ[q], lambda: norm(2, SEQ[q - 1]))
                    norm(2, SEQ[-1])
                    dve.wait_ge(f_xTc, 2 + 2 * PAIRS)
                    nc.vector.reduce_sum(csum, x_sums, AX.X).then_inc(f_cs, 1)

        with nc.Block() as block:
            @block.gpsimd
            def _(pool):
                full = pool.value_load(bad_i[0:1, 0:1], min_val=0, max_val=1)
                with pool.If(full == 0):
                    fast_gpsimd(pool)

            @block.sync
            def _(sp):
                full = sp.value_load(bad_i[0:1, 0:1], min_val=0, max_val=1)
                with sp.If(full == 0):
                    fast_sync(sp)
                with sp.Else():
                    dense_sync(sp)

            @block.tensor
            def _(pe):
                full = pe.value_load(bad_i[0:1, 0:1], min_val=0, max_val=1)
                with pe.If(full == 0):
                    fast_tensor(pe)
                with pe.Else():
                    dense_tensor(pe)

            @block.scalar
            def _(act):
                full = act.value_load(bad_i[0:1, 0:1], min_val=0, max_val=1)
                with act.If(full == 0):
                    fast_scalar(act)
                with act.Else():
                    dense_scalar(act)

            @block.vector
            def _(dve):
                full = dve.value_load(bad_i[0:1, 0:1], min_val=0, max_val=1)
                with dve.If(full == 0):
                    fast_vector(dve)
                with dve.Else():
                    dense_vector(dve)


_INS = ['x', 'adj', 'L0_gnn_attn', 'L1_gnn_W', 'L1_gnn_a', 'L2_gnn_W', 'L2_gnn_a', 'L3_gnn_W', 'L3_gnn_a']
_OUTS = [((8192, 128), 'float32')]


def kernel(**inputs):
    import numpy as _np
    import concourse.bacc as _bacc
    from concourse import mybir as _mybir
    from concourse.bass_utils import run_bass_kernel_spmd as _run

    nc = _bacc.Bacc("TRN2", target_bir_lowering=False, num_devices=1)
    arrays, args = {}, []
    for name in _INS:
        a = _np.ascontiguousarray(inputs[name])
        arrays[f"in_{name}_dram"] = a
        args.append(nc.dram_tensor(f"in_{name}_dram", a.shape, _mybir.dt.from_np(a.dtype), kind="ExternalInput").ap())
    for i, (shape, dtype) in enumerate(_OUTS):
        dt = _mybir.dt.from_np(_np.dtype(dtype))
        args.append(nc.dram_tensor(f"out_{i}_dram", shape, dt, kind="ExternalOutput").ap())
    build_program(nc, *args)
    r = _run(nc, [arrays], core_ids=[0])
    got = tuple(r.results[0][f"out_{i}_dram"] for i in range(len(_OUTS)))
    return got[0]
```
